# Optimizing a Trainium2 kernel written in Bass

```python
import numpy as np
import jax
import jax.numpy as jnp

def _softmax(x, axis=-1):
    return jax.nn.softmax(x, axis=axis)

def _gelu(x):
    return jax.nn.gelu(x, approximate=True)

def _silu(x):
    return jax.nn.silu(x)

def _sigmoid(x):
    return jax.nn.sigmoid(x)

def _layernorm(x, axis=-1, eps=1e-05):
    m = jnp.mean(x, axis=axis, keepdims=True)
    v = jnp.var(x, axis=axis, keepdims=True)
    return (x - m) / jnp.sqrt(v + eps)

def _scatter_add(tgt, idx, src, axis=0):
    return tgt.at[idx].add(src)

def _segment_sum(src, seg, n):
    return jax.ops.segment_sum(src, seg, n)
kernel_name = 'mk_gnn_resnorm_d2_gnn_r32_1cd0ec'

def setup_inputs(seed: int=0):
    np.random.seed(seed)
    _w = jnp.asarray

    def _rec_inputs():
        import jax
        import jax.numpy as jnp
        _gk = jax.random.key(seed)
        x = -0.0003713 + 1 * jax.random.normal(jax.random.fold_in(_gk, 1), (3125, 128), jnp.float32)
        src = jax.random.randint(jax.random.fold_in(_gk, 2), (100000,), 0, 3125, jnp.int32)
        dst = jax.random.randint(jax.random.fold_in(_gk, 3), (100000,), 0, 3125, jnp.int32)
        _o = jnp.argsort(dst, stable=True)
        src = src[_o]
        dst = dst[_o]
        edge_weight = jax.random.uniform(jax.random.fold_in(_gk, 13), (100000,), jnp.float32, 0.0, 1)
        return (x, src, dst, edge_weight)
    x, src, dst, edge_weight = _rec_inputs()

    def _L0_gnn_setup():
        import jax, jax.numpy as jnp
        import numpy as np
        N_NODES = 3125
        N_EDGES = 20000
        D = 128
        L = 2

        def _layer_norm(h, g, b, eps=1e-05):
            mu = jnp.mean(h, axis=-1, keepdims=True)
            var = jnp.mean((h - mu) ** 2, axis=-1, keepdims=True)
            return (h - mu) * jax.lax.rsqrt(var + eps) * g + b
        key = jax.random.key(seed)
        ks = jax.random.split(key, 8)
        s = 1.0 / np.sqrt(D)
        return {'x': jax.random.normal(ks[0], (N_NODES, D), jnp.float32), 'edge_index': jax.random.randint(ks[1], (2, N_EDGES), 0, N_NODES, jnp.int32), 'Ws': jax.random.normal(ks[2], (L, D, D), jnp.float32) * s, 'bs': jax.random.normal(ks[3], (L, D), jnp.float32) * s, 'Wn': jax.random.normal(ks[4], (L, D, D), jnp.float32) * s, 'bn': jax.random.normal(ks[5], (L, D), jnp.float32) * s, 'Wa': jax.random.normal(ks[6], (L, 2 * D), jnp.float32) * s, 'ba': jax.random.normal(ks[7], (L,), jnp.float32) * s, 'gamma': jnp.ones((L, D), jnp.float32), 'beta': jnp.zeros((L, D), jnp.float32)}
    _L0_gnn_all = _L0_gnn_setup()
    _L0_gnn_in = {k: v for k, v in _L0_gnn_all.items() if k in ('Ws', 'bs', 'Wn', 'bn', 'Wa', 'ba', 'gamma', 'beta')}
    del _L0_gnn_all

    def _L1_gnn_setup():
        import jax, jax.numpy as jnp
        import numpy as np
        N = 3125
        E = 100000
        F_IN = 128
        C = 128
        key = jax.random.key(seed)
        k1, k2, k3, k4, k5, k6 = jax.random.split(key, 6)
        features = jax.random.normal(k1, (N, F_IN), dtype=jnp.float32)
        kernel = jax.random.normal(k2, (F_IN, C), dtype=jnp.float32) * (1.0 / np.sqrt(F_IN))
        bias = jax.random.normal(k3, (C,), dtype=jnp.float32) * 0.01
        edge_vals = jax.random.uniform(k4, (E,), dtype=jnp.float32)
        edge_row = jnp.sort(jax.random.randint(k5, (E,), 0, N, dtype=jnp.int32))
        edge_col = jax.random.randint(k6, (E,), 0, N, dtype=jnp.int32)
        return {'features': features, 'kernel': kernel, 'bias': bias, 'edge_vals': edge_vals, 'edge_row': edge_row, 'edge_col': edge_col}
    _L1_gnn_all = _L1_gnn_setup()
    _L1_gnn_in = {k: v for k, v in _L1_gnn_all.items() if k in ('kernel', 'bias')}
    del _L1_gnn_all
    return {'x': x, 'src': src, 'dst': dst, 'edge_weight': edge_weight, 'L0_gnn_Ws': _L0_gnn_in['Ws'], 'L0_gnn_bs': _L0_gnn_in['bs'], 'L0_gnn_Wn': _L0_gnn_in['Wn'], 'L0_gnn_bn': _L0_gnn_in['bn'], 'L0_gnn_Wa': _L0_gnn_in['Wa'], 'L0_gnn_ba': _L0_gnn_in['ba'], 'L0_gnn_gamma': _L0_gnn_in['gamma'], 'L0_gnn_beta': _L0_gnn_in['beta'], 'L1_gnn_kernel': _L1_gnn_in['kernel'], 'L1_gnn_bias': _L1_gnn_in['bias']}

def reference(x, src, dst, edge_weight, L0_gnn_Ws, L0_gnn_bs, L0_gnn_Wn, L0_gnn_bn, L0_gnn_Wa, L0_gnn_ba, L0_gnn_gamma, L0_gnn_beta, L1_gnn_kernel, L1_gnn_bias):
    import jax
    import jax.numpy as jnp

    def _L0_gnn_ref(x, edge_index, Ws, bs, Wn, bn, Wa, ba, gamma, beta):
        import jax, jax.numpy as jnp
        import numpy as np
        N_NODES = 3125
        N_EDGES = 20000
        D = 128
        L = 2

        def _layer_norm(h, g, b, eps=1e-05):
            mu = jnp.mean(h, axis=-1, keepdims=True)
            var = jnp.mean((h - mu) ** 2, axis=-1, keepdims=True)
            return (h - mu) * jax.lax.rsqrt(var + eps) * g + b
        num_nodes = x.shape[0]
        row, col = (edge_index[0], edge_index[1])
        for l in range(L):
            out_self = x @ Ws[l] + bs[l]
            neigh = x[row] @ Wn[l] + bn[l]
            logits = x[col] @ Wa[l, :D] + neigh @ Wa[l, D:] + ba[l]
            score = jax.nn.sigmoid(logits)[:, None]
            agg = jax.ops.segment_sum(neigh * score, col, num_segments=num_nodes)
            ssum = jax.ops.segment_sum(score, col, num_segments=num_nodes)
            h = jax.nn.gelu(out_self + agg / (ssum + 1e-06), approximate=False) + x
            x = _layer_norm(h, gamma[l], beta[l])
        return x

    def _L1_gnn_ref(features, kernel, bias, edge_vals, edge_row, edge_col):
        import jax, jax.numpy as jnp
        import numpy as np
        N = 3125
        E = 100000
        F_IN = 128
        C = 128
        h = features @ kernel
        msgs = edge_vals[:, None] * h[edge_col]
        out = jax.ops.segment_sum(msgs, edge_row, num_segments=features.shape[0])
        return jax.nn.relu(out + bias)
    edge_index = jnp.stack([src, dst])
    x = _layernorm(x + _L0_gnn_ref(x, edge_index, L0_gnn_Ws, L0_gnn_bs, L0_gnn_Wn, L0_gnn_bn, L0_gnn_Wa, L0_gnn_ba, L0_gnn_gamma, L0_gnn_beta), axis=-1)
    x = _layernorm(x + _L1_gnn_ref(x, L1_gnn_kernel, L1_gnn_bias, edge_weight, src, dst), axis=-1)
    return x

_drawn_inputs = setup_inputs


def setup_inputs(seed=0):
    import zlib

    import numpy as np

    out = dict(_drawn_inputs(seed))
    spreads = {'L0_gnn_gamma': (1.0, 0.2), 'L0_gnn_beta': (0.0, 0.1)}
    factors = {'L0_gnn_ba': 8.0, 'L1_gnn_bias': 8.0}
    for name, (base, spread) in spreads.items():
        noise = np.random.default_rng([zlib.crc32(name.encode()), seed]).standard_normal(out[name].shape)
        drawn = base * np.exp(spread * noise) if base else spread * noise
        out[name] = jnp.asarray(drawn.astype(out[name].dtype))
    for name, factor in factors.items():
        out[name] = (out[name] * factor).astype(out[name].dtype)
    return out
```

```python
from contextlib import ExitStack

import concourse.bass as bass
from concourse import mybir

ALU = mybir.AluOpType
ACT = mybir.ActivationFunctionType
AX = mybir.AxisListType
F32 = mybir.dt.float32
I32 = mybir.dt.int32

EPS_NORM = 1e-5
EPS_SCORE = 1e-6
ROUND = float(3 << 22)


def gnn_kernel(nc, x, src, dst, edge_weight, Ws, bs, Wn, bn, Wa, ba, gamma, beta, kernel1, bias1, out):
    N, D = x.shape
    E = src.shape[0]
    L = Ws.shape[0]
    P = 125
    T = N // P
    K = E // P
    assert N == P * T and E == P * K and D == 128
    W = 2 * D + 2
    NEIGH, B, SELF, A = 0, D, D + 1, 2 * D + 1
    PER_BANK = 4
    GROUPS = -(-T // PER_BANK)
    PASSES = L + 1

    with ExitStack() as ctx:
        def sb(name, shape, dt=F32):
            return ctx.enter_context(nc.sbuf_tensor(name, shape, dt))

        def sem(name):
            return ctx.enter_context(nc.semaphore(name))

        ps = ctx.enter_context(nc.psum_tensor("ps", [128, 8, 512], F32))
        x0 = sb("x0", [P, T, D])
        xs = sb("xs", [P, T, D])
        xT = sb("xT", [D, T, P])
        NB = sb("NB", [P, T, W])
        AG = sb("AG", [P, T, D + 1])
        wide = sb("wide", [D, L, W])
        kern = sb("kern", [D, D])
        biasw = sb("biasw", [P, L, W])
        wa2 = sb("wa2", [D, L, D])
        prod = sb("prod", [D, D])
        gam = sb("gam", [P, L, D])
        bet = sb("bet", [P, L, D])
        bi1 = sb("bi1", [P, D])
        src_i = sb("src_i", [P, K], I32)
        dst_i = sb("dst_i", [P, K], I32)
        wgt = sb("wgt", [P, K])
        src_hl = sb("src_hl", [P, 2, K])
        dst_hl = sb("dst_hl", [P, 2, K])
        tmp = sb("tmp", [P, T, D])
        st = sb("st", [P, 4, T])
        a_col = sb("a_col", [P, T])
        iota_i = sb("iota_i", [P, D], I32)
        iota = sb("iota", [P, D])
        part_i = sb("part_i", [P, 1], I32)
        part = sb("part", [P, 1])
        ident = sb("ident", [P, P])
        gidx = sb("gidx", [P, 1], I32)
        aidx = sb("aidx", [P, 1], I32)
        rows = sb("rows", [P, D + 1])
        a_dst = sb("a_dst", [P, 1])
        score = sb("score", [P, 1])
        oh_hi = sb("oh_hi", [P, P])
        oh_lo = sb("oh_lo", [P, T])
        oh_s = sb("oh_s", [P, T])
        onehot = sb("onehot", [P, T, P])
        pool_idx = sb("pool_idx", [P, 1], I32)
        msg = sb("msg", [P, D])

        table = nc.dram_tensor("node_table", [N, D + 1], F32).ap()
        a_table = nc.dram_tensor("a_table", [N, 1], F32).ap()

        s_x = sem("s_x")
        s_w = sem("s_w")
        s_e = sem("s_e")
        s_iota = sem("s_iota")
        s_ident = sem("s_ident")
        s_wide = sem("s_wide")
        s_edges = sem("s_edges")
        s_v = sem("s_v")
        s_xt = sem("s_xt")
        s_xtc = sem("s_xtc")
        s_nb = sem("s_nb")
        s_nbc = sem("s_nbc")
        s_acol = sem("s_acol")
        s_tab = sem("s_tab")
        g_idx = [sem(f"g_idx{l}") for l in range(PASSES)]
        g_rows = [sem(f"g_rows{l}") for l in range(PASSES)]
        g_score = [sem(f"g_score{l}") for l in range(PASSES)]
        g_oh = [sem(f"g_oh{l}") for l in range(PASSES)]
        g_msg = [sem(f"g_msg{l}") for l in range(PASSES)]
        g_used = [sem(f"g_used{l}") for l in range(PASSES)]
        g_hot = [sem(f"g_hot{l}") for l in range(PASSES)]
        g_pad = [sem(f"g_pad{l}") for l in range(PASSES)]
        s_pre = sem("s_pre")
        s_gelu = sem("s_gelu")
        s_cen = sem("s_cen")
        s_sq = sem("s_sq")
        s_var = sem("s_var")
        s_std = sem("s_std")
        s_new = sem("s_new")
        s_out = sem("s_out")

        NDMA_W = 0
        block = ctx.enter_context(nc.Block())
        x_dram = x.rearrange("(p t) d -> p t d", t=T)
        out_dram = out.rearrange("(p t) d -> p t d", t=T)

        @block.sync
        def _(sp):
            sp.dma_start(x0[:], x_dram).then_inc(s_x, 16)
            sp.dma_start(xs[:], x_dram).then_inc(s_x, 16)
            for l in range(L):
                sp.dma_start(wide[:, l, NEIGH:NEIGH + D], Wn[l]).then_inc(s_w, 16)
                sp.dma_start(wide[:, l, SELF:SELF + D], Ws[l]).then_inc(s_w, 16)
                sp.dma_start(wide[:, l, A:A + 1], Wa[l, 0:D].unsqueeze(1)).then_inc(s_w, 16)
                sp.dma_start(wa2[:, l, :], Wa[l, D:2 * D].partition_broadcast(D)).then_inc(s_w, 16)
                sp.dma_start(biasw[:, l, NEIGH:NEIGH + D], bn[l].partition_broadcast(P)).then_inc(s_w, 16)
                sp.dma_start(biasw[:, l, SELF:SELF + D], bs[l].partition_broadcast(P)).then_inc(s_w, 16)
                sp.dma_start(biasw[:, l, A:A + 1], ba[l:l + 1].partition_broadcast(P)).then_inc(s_w, 16)
                sp.dma_start(gam[:, l, :], gamma[l].partition_broadcast(P)).then_inc(s_w, 16)
                sp.dma_start(bet[:, l, :], beta[l].partition_broadcast(P)).then_inc(s_w, 16)
            sp.dma_start(kern[:], kernel1).then_inc(s_w, 16)
            sp.dma_start(bi1[:], bias1.partition_broadcast(P)).then_inc(s_w, 16)
            sp.dma_start(src_i[:], src.rearrange("(p k) -> p k", k=K)).then_inc(s_e, 16)
            sp.dma_start(dst_i[:], dst.rearrange("(p k) -> p k", k=K)).then_inc(s_e, 16)
            sp.dma_start(wgt[:], edge_weight.rearrange("(p k) -> p k", k=K)).then_inc(s_e, 16)
            for l in range(PASSES):
                sp.wait_ge(s_nbc, T * (l + 1))
                sp.dma_start(table.rearrange("(p t) d -> p t d", t=T), NB[:, :, 0:D + 1]).then_inc(s_tab, 16)
                if l < L:
                    sp.wait_ge(s_acol, l + 1)
                    sp.dma_start(a_table.rearrange("(p t) d -> p (t d)", t=T), a_col[:]).then_inc(s_tab, 16)
            sp.wait_ge(s_new, PASSES + 1)
            sp.dma_start(out_dram, xs[:]).then_inc(s_out, 16)
            sp.wait_ge(s_out, 16)
            sp.wait_ge(s_tab, 16 * (2 * L + 1))

        W_LOADED = 16 * (9 * L + 2)

        @block.gpsimd
        def _(pool):
            nc.gpsimd.iota(iota_i[:], pattern=[[1, D]], base=0, channel_multiplier=0).then_inc(s_iota, 1)
            nc.gpsimd.iota(part_i[:], pattern=[[0, 1]], base=0, channel_multiplier=1).then_inc(s_iota, 1)
            for l in range(PASSES):
                pool.wait_ge(s_tab, 16 * min(2 * (l + 1), 2 * L + 1))
                per = 32 if l < L else 16
                with pool.Fori(0, K) as k:
                    pool.wait_ge(g_idx[l], 2 * k + 2)
                    pool.wait_ge(g_msg[l], k + 1)
                    pool.sem_inc(g_pad[l],1)
                    pool.indirect_dma_start(rows[:], None, table, bass.IndirectOffsetOnAxis(gidx[:], 0)).then_inc(g_rows[l], 16)
                    if l < L:
                        pool.indirect_dma_start(a_dst[:], None, a_table, bass.IndirectOffsetOnAxis(aidx[:], 0)).then_inc(g_rows[l], 16)

        @block.tensor
        def _(pe):
            pe.wait_ge(s_ident, 1)
            for l in range(PASSES):
                if l == 0:
                    pe.wait_ge(s_x, 32)
                else:
                    pe.wait_ge(s_new, l)
                for g in range(GROUPS):
                    tiles = range(g * PER_BANK, min(T, (g + 1) * PER_BANK))
                    for t in tiles:
                        last = pe.transpose(ps[:, g, (t % PER_BANK) * P:(t % PER_BANK + 1) * P], xs[:, t, :], ident[:])
                    last.then_inc(s_xt, 1)
                pe.wait_ge(s_w, W_LOADED)
                pe.wait_ge(s_wide, 2 * L)
                for t in range(T):
                    pe.wait_ge(s_xtc, l * GROUPS + max(t // PER_BANK, min(t, GROUPS - 1)) + 1)
                    if t >= 8:
                        pe.wait_ge(s_nbc, l * T + t - 7)
                    if l < L:
                        pe.matmul(ps[0:P, t % 8, 0:W], xT[:, t, :], wide[:, l, :], start=True, stop=True).then_inc(s_nb, 1)
                    else:
                        pe.matmul(ps[0:P, t % 8, 0:D], xT[:, t, :], kern[:], start=True, stop=True).then_inc(s_nb, 1)

                def chunk(k, first):
                    pe.wait_ge(g_oh[l], k + 1)
                    pe.wait_ge(g_msg[l], k + 2)
                    for t in range(T):
                        last = pe.matmul(ps[0:P, t // PER_BANK, (t % PER_BANK) * D:(t % PER_BANK + 1) * D], onehot[:, t, :], msg[:],
                                         start=(first and t % PER_BANK == 0), stop=False, skip_group_check=True)
                    if l < L:
                        last = pe.matmul(ps[0:P, 7, 0:T], oh_hi[:], oh_s[:], start=first, stop=False, skip_group_check=True)
                    last.then_inc(g_used[l], 1)

                pe.sem_inc(g_used[l], 1)
                pe.wait_ge(s_nbc, (l + 1) * T)
                chunk(0, True)
                with pe.Fori(1, K) as k:
                    chunk(k, False)

        @block.scalar
        def _(act):
            for l in range(PASSES):
                for g in range(1, GROUPS, 2):
                    n = min(T, (g + 1) * PER_BANK) - g * PER_BANK
                    act.wait_ge(s_xt, l * GROUPS + g + 1)
                    act.wait_ge(s_xtc, l * GROUPS + g)
                    nc.scalar.copy(xT[:, g * PER_BANK:g * PER_BANK + n, :], ps[:, g, 0:n * P].rearrange("q (t p) -> q t p", p=P)).then_inc(s_xtc, 1)
                if l < L:
                    with act.Fori(0, K) as k:
                        act.wait_ge(g_rows[l], 32 * k + 32)
                        nc.scalar.activation(score[:], rows[:, D:D + 1], ACT.Sigmoid, bias=a_dst[:]).then_inc(g_score[l], 1)
                    act.wait_ge(s_pre, l + 1)
                    nc.scalar.activation(tmp[:], tmp[:], ACT.Gelu).then_inc(s_gelu, 1)
                for n in range(2 if l == L - 1 else 1):
                    i = l + n + (1 if l == L else 0)
                    act.wait_ge(s_cen, i + 1)
                    nc.scalar.activation(AG[:, :, 0:D], xs[:], ACT.Square).then_inc(s_sq, 1)
                    act.wait_ge(s_var, i + 1)
                    nc.scalar.activation(st[:, 2, :], st[:, 1, :], ACT.Sqrt).then_inc(s_std, 1)

        @block.vector
        def _(dve):
            steps = [0]

            def link(ins):
                ins.then_inc(s_v, 1)
                steps[0] += 1
                dve.wait_ge(s_v, steps[0])

            def spread(v):
                return v.unsqueeze(2).to_broadcast([P, T, D])

            def along(v):
                return v.unsqueeze(1).to_broadcast([P, T, D])

            dve.wait_ge(s_iota, 2)
            link(nc.vector.tensor_copy(iota[:], iota_i[:]))
            link(nc.vector.tensor_copy(part[:], part_i[:]))
            nc.vector.tensor_scalar(ident[:], iota[:, 0:P], part[:], None, ALU.is_equal).then_inc(s_ident, 1)
            dve.wait_ge(s_w, W_LOADED)
            for l in range(L):
                link(nc.vector.tensor_tensor_reduce(prod[:], wide[:, l, NEIGH:NEIGH + D], wa2[:, l, :], 1.0, 0.0, ALU.mult, ALU.add, wide[:, l, B:B + 1]))
                link(nc.vector.tensor_tensor_reduce(prod[0:P], biasw[:, l, NEIGH:NEIGH + D], wa2[0:P, l, :], 1.0, 0.0, ALU.mult, ALU.add, biasw[:, l, B:B + 1]))
                dve.sem_inc(s_wide, 2)
            dve.wait_ge(s_e, 48)
            for ids, hl in ((src_i, src_hl), (dst_i, dst_hl)):
                link(nc.vector.tensor_copy(hl[:, 1, :], ids[:]))
                link(nc.vector.tensor_scalar(hl[:, 0, :], hl[:, 1, :], -(T - 1) / 2, 1.0 / T, ALU.add, ALU.mult))
                link(nc.vector.tensor_scalar(hl[:, 0, :], hl[:, 0, :], ROUND, None, ALU.add))
                link(nc.vector.tensor_scalar(hl[:, 0, :], hl[:, 0, :], -ROUND, None, ALU.add))
                link(nc.vector.scalar_tensor_tensor(hl[:, 1, :], hl[:, 0, :], -float(T), hl[:, 1, :], ALU.mult, ALU.add))

            for l in range(PASSES):
                for g in range(0, GROUPS, 2):
                    n = min(T, (g + 1) * PER_BANK) - g * PER_BANK
                    dve.wait_ge(s_xt, l * GROUPS + g + 1)
                    if g:
                        dve.wait_ge(s_xtc, l * GROUPS + g)
                    nc.vector.tensor_copy(xT[:, g * PER_BANK:g * PER_BANK + n, :], ps[:, g, 0:n * P].rearrange("q (t p) -> q t p", p=P)).then_inc(s_xtc, 1)
                for t in range(T):
                    dve.wait_ge(s_nb, l * T + t + 1)
                    if l < L:
                        nc.vector.tensor_tensor(NB[:, t, :], ps[0:P, t % 8, 0:W], biasw[:, l, :], ALU.add).then_inc(s_nbc, 1)
                    else:
                        nc.vector.tensor_copy(NB[:, t, 0:D], ps[0:P, t % 8, 0:D]).then_inc(s_nbc, 1)
                dve.wait_ge(s_nbc, T * (l + 1))
                if l < L:
                    nc.vector.tensor_copy(a_col[:], NB[:, :, A]).then_inc(s_acol, 1)

                g_i, o_hl = (src_i, dst_hl) if l < L else (dst_i, src_hl)
                dve.sem_inc(g_msg[l], 1)
                with dve.Fori(0, K) as k:
                    nc.vector.tensor_copy(gidx[:], g_i[:, bass.ds(k, 1)]).then_inc(g_idx[l], 1)
                    nc.vector.tensor_copy(aidx[:], dst_i[:, bass.ds(k, 1)]).then_inc(g_idx[l], 1)
                    dve.wait_ge(g_used[l], k + 1)
                    nc.vector.tensor_scalar(oh_hi[:], iota[:, 0:P], o_hl[:, 0, bass.ds(k, 1)], None, ALU.is_equal).then_inc(g_hot[l], 1)
                    nc.vector.tensor_scalar(oh_lo[:], iota[:, 0:T], o_hl[:, 1, bass.ds(k, 1)], None, ALU.is_equal).then_inc(g_hot[l], 1)
                    dve.wait_ge(g_hot[l], 2 * k + 2)
                    nc.vector.tensor_tensor(onehot[:], oh_hi[:].unsqueeze(1).to_broadcast([P, T, P]), oh_lo[:].unsqueeze(2).to_broadcast([P, T, P]), ALU.mult).then_inc(g_oh[l], 1)
                    if l < L:
                        dve.wait_ge(g_score[l], k + 1)
                        nc.vector.tensor_scalar(oh_s[:], oh_lo[:], score[:], None, ALU.mult)
                        nc.vector.tensor_scalar(msg[:], rows[:, 0:D], score[:], None, ALU.mult).then_inc(g_msg[l], 1)
                    else:
                        dve.wait_ge(g_rows[l], 16 * k + 16)
                        nc.vector.tensor_scalar(msg[:], rows[:, 0:D], wgt[:, bass.ds(k, 1)], None, ALU.mult).then_inc(g_msg[l], 1)
                dve.wait_ge(g_used[l], K + 1)
                for g in range(GROUPS):
                    n = min(T, (g + 1) * PER_BANK) - g * PER_BANK
                    link(nc.vector.tensor_copy(AG[:, g * PER_BANK:g * PER_BANK + n, 0:D], ps[0:P, g, 0:n * D].rearrange("p (t d) -> p t d", d=D)))
                if l < L:
                    link(nc.vector.tensor_scalar(st[:, 0, :], ps[0:P, 7, 0:T], EPS_SCORE, None, ALU.add))
                    link(nc.vector.reciprocal(st[:, 0, :], st[:, 0, :]))
                    link(nc.vector.tensor_tensor(tmp[:], AG[:, :, 0:D], spread(st[:, 0, :]), ALU.mult))
                    link(nc.vector.tensor_tensor(tmp[:], tmp[:], NB[:, :, SELF:SELF + D], ALU.add))
                    dve.sem_inc(s_pre, 1)
                    dve.wait_ge(s_gelu, l + 1)
                    link(nc.vector.tensor_tensor(xs[:], xs[:], tmp[:], ALU.add))
                else:
                    link(nc.vector.tensor_tensor(tmp[:], AG[:, :, 0:D], along(bi1[:]), ALU.add))
                    link(nc.vector.tensor_scalar(tmp[:], tmp[:], 0.0, None, ALU.max))
                    link(nc.vector.tensor_tensor(xs[:], xs[:], tmp[:], ALU.add))

                for n in range(2 if l == L - 1 else 1):
                    i = l + n + (1 if l == L else 0)
                    affine = l < L and n == 0
                    if n:
                        link(nc.vector.tensor_tensor(xs[:], xs[:], x0[:], ALU.add))
                    link(nc.vector.tensor_reduce(st[:, 0, :], xs[:], AX.X, ALU.add))
                    link(nc.vector.tensor_scalar(st[:, 0, :], st[:, 0, :], -1.0 / D, None, ALU.mult))
                    nc.vector.tensor_tensor(xs[:], xs[:], spread(st[:, 0, :]), ALU.add).then_inc(s_cen, 1)
                    dve.wait_ge(s_sq, i + 1)
                    link(nc.vector.tensor_reduce(st[:, 1, :], AG[:, :, 0:D], AX.X, ALU.add))
                    nc.vector.tensor_scalar(st[:, 1, :], st[:, 1, :], 1.0 / D, EPS_NORM, ALU.mult, ALU.add).then_inc(s_var, 1)
                    dve.wait_ge(s_std, i + 1)
                    link(nc.vector.reciprocal(st[:, 0, :], st[:, 2, :]))
                    ins = nc.vector.tensor_tensor(xs[:], xs[:], spread(st[:, 0, :]), ALU.mult)
                    if affine:
                        link(ins)
                        link(nc.vector.tensor_tensor(xs[:], xs[:], along(gam[:, l, :]), ALU.mult))
                        ins = nc.vector.tensor_tensor(xs[:], xs[:], along(bet[:, l, :]), ALU.add)
                    if l == L - 1 and n == 0:
                        link(ins)
                    else:
                        ins.then_inc(s_new, 2 if l == L else 1)
                        dve.wait_ge(s_new, PASSES + 1 if l == L else l + 1)


_INS = ['x', 'src', 'dst', 'edge_weight', 'L0_gnn_Ws', 'L0_gnn_bs', 'L0_gnn_Wn', 'L0_gnn_bn', 'L0_gnn_Wa', 'L0_gnn_ba',
        'L0_gnn_gamma', 'L0_gnn_beta', 'L1_gnn_kernel', 'L1_gnn_bias']


def kernel(**inputs):
    import numpy as _np
    import concourse.bacc as _bacc
    from concourse import mybir as _mybir
    from concourse.bass_utils import run_bass_kernel_spmd as _run

    nc = _bacc.Bacc("TRN2", target_bir_lowering=False, num_devices=1)
    arrays, args = {}, []
    for name in _INS:
        a = _np.ascontiguousarray(inputs[name])
        arrays[f"in_{name}_dram"] = a
        args.append(nc.dram_tensor(f"in_{name}_dram", a.shape, _mybir.dt.from_np(a.dtype), kind="ExternalInput").ap())
    out = nc.dram_tensor("out_dram", (3125, 128), _mybir.dt.float32, kind="ExternalOutput").ap()
    gnn_kernel(nc, *args, out)
    r = _run(nc, [arrays], core_ids=[0])
    return r.results[0]["out_dram"]
```

```python
from contextlib import ExitStack

import concourse.bass as bass
from concourse import mybir

ALU = mybir.AluOpType
ACT = mybir.ActivationFunctionType
AX = mybir.AxisListType
F32 = mybir.dt.float32
F16 = mybir.dt.float16
BF16 = mybir.dt.bfloat16
I32 = mybir.dt.int32
U8 = mybir.dt.uint8

EPS_NORM = 1e-5
EPS_SCORE = 1e-6
ROUND = float(3 << 22)



def gnn_kernel(nc, x, src, dst, edge_weight, Ws, bs, Wn, bn, Wa, ba, gamma, beta, kernel1, bias1, out, all_edges=None):
    N, D = x.shape
    E = src.shape[0]
    L = Ws.shape[0]
    P = 125
    T = N // P
    K = E // P
    assert N == P * T and E == P * K and D == 128
    PASSES = L + 1
    all_edges = E if all_edges is None else all_edges

    PER_BANK = 4
    BANKFULS = -(-T // PER_BANK)
    NW = D + 2
    ONE, B = D, D + 1

    WIN = 2
    GW = 25
    GP = 26
    KEYS = WIN * T
    COLS = -(-N // (WIN * P))
    GROUPS = -(-N // (WIN * GW))
    SLOTS = 128
    BLOCK = 32
    NBLK = E // BLOCK
    LASTB = (E - SLOTS) // BLOCK
    SPLIT = [(0, 10), (10, 20), (20, 25)]
    CW = COLS * P * WIN
    GC = GW * WIN
    JT = 5
    JC = JT * P

    with ExitStack() as ctx:
        def sb(name, shape, dt=F32):
            return ctx.enter_context(nc.sbuf_tensor(name, shape, dt))

        def sem(name):
            return ctx.enter_context(nc.semaphore(name))

        ps = ctx.enter_context(nc.psum_tensor("ps", [128, 8, 512], F32))

        xs = sb("xs", [P, T, D])
        xa = sb("xa", [128, T * (D + 1)])
        nb = sb("nb", [128, 4056])
        so = sb("so", [P, T, D])
        ab = sb("ab", [P, T * D])
        edgesT = sb("edgesT", [128, 5, COLS * 5 * GP], BF16)
        hot = sb("hot", [128, 2, P + KEYS, GP], BF16)
        iota_rep = sb("iota_rep", [128, P, GP], BF16)
        arena = sb("arena", [128, 20352])
        wideN = sb("wideN", [D, L, NW])
        wideS = sb("wideS", [D, L, D])
        wa1 = sb("wa1", [D, L])
        wa1_rep = sb("wa1_rep", [D, L, P])
        kern = sb("kern", [D, D])
        biasN = sb("biasN", [P, L, NW])
        biasS = sb("biasS", [P, L, D])
        ba_b = sb("ba_b", [P, L])
        gam = sb("gam", [P, L, D])
        bet = sb("bet", [P, L, D])
        bi1 = sb("bi1", [P, D])
        st = sb("st", [P, 3, T])
        ident = sb("ident", [P, P])
        ident16 = sb("ident16", [P, P], BF16)
        ones = sb("ones", [P, 1])
        ones16 = sb("ones16", [P, 1], BF16)
        part = sb("part", [P, 1])
        caught = sb("caught", [P, 1])
        fast_i = sb("fast_i", [1, 1], I32)

        xT = xa[:, 0:N]
        agg = xa[0:P, :].rearrange("p (t d) -> p t d", d=D + 1)
        accum = xa[0:P, 0:T * D].rearrange("p (t d) -> p t d", d=D)
        NB = nb[0:P, 0:T * NW].rearrange("p (t d) -> p t d", d=NW)
        x_in = nb[0:P, 0:T * D].rearrange("p (t d) -> p t d", d=D)
        KW = nb[:, 0:3 * KEYS * GP].bitcast(BF16).rearrange("q (s j k w) -> q s j k w", s=2, j=3, w=GP)
        tmp = ab[:].rearrange("p (t d) -> p t d", d=D)
        HI = hot[:, :, 0:P, :]
        KEY = hot[:, :, P:P + KEYS, :]
        hotf = hot[:].rearrange("q s v w -> q (s v w)").bitcast(F32)
        S = [hotf[0:P, j * JC:(j + 1) * JC] for j in range(2)]
        PR = [hotf[0:P, (2 + j) * JC:(3 + j) * JC] for j in range(2)]

        flat = arena[:]

        class Carve:
            def __init__(self):
                self.at = 0

            def __call__(self, parts, n):
                self.at += n
                assert self.at <= 20352
                return flat[0:parts, self.at - n:self.at]

        cmp_ = flat[0:P, 0:T * COLS * P // 2 + 1].bitcast(BF16)[:, 0:T * COLS * P].rearrange("p (b w) -> p b w", b=T)
        cut = Carve()
        fetched = cut(P, COLS * 3 * SLOTS).bitcast(I32).rearrange("p (c f e) -> p c f e", c=COLS, f=3)
        e_f = [cut(P, COLS * SLOTS).rearrange("p (c e) -> p c e", c=COLS) for _ in range(4)]
        e_16 = [cut(P, COLS * SLOTS // 2).bitcast(BF16).rearrange("p (c e) -> p c e", c=COLS) for _ in range(5)]
        C = flat[0:P, 0:-(-T * CW // 4)].bitcast(U8)[:, 0:T * CW].rearrange("p (r c) -> p r c", r=T)
        cut = Carve()
        W = [cut(P, T * 2 * P).rearrange("p (r c) -> p r c", r=T) for _ in range(2)]
        WT = [cut(P, T * P).rearrange("p (r q) -> p r q", r=T) for _ in range(2)]
        cut = Carve()
        src_i = cut(P, K).bitcast(I32)
        dst_i = cut(P, K).bitcast(I32)
        wgt = cut(P, K)
        src_hl = cut(P, 2 * K).rearrange("p (j k) -> p j k", j=2)
        dst_tl = cut(P, 2 * K).rearrange("p (j k) -> p j k", j=2)
        onehot = cut(P, T * P).rearrange("p (t q) -> p t q", t=T)
        oh_row = cut(P, P)
        oh_blk = cut(P, T)
        oh_s = cut(P, T)
        msg = cut(P, D)
        rows = cut(P, NW)
        a_dst = cut(P, 1)
        score = cut(P, 1)
        gidx = cut(P, 1).bitcast(I32)
        aidx = cut(P, 1).bitcast(I32)
        iota_f = sb("iota_f", [P, D])
        small_i = sb("small_i", [P, D], I32)
        part_i = sb("part_i", [P, 1], I32)
        wa2 = sb("wa2", [D, L, D])
        prod = sb("prod", [D, D])
        wins = ab[:, 0:COLS * P // 2 + 1].bitcast(F16)[:, 0:COLS * P]
        win_i = sb("win_i", [P, COLS], I32)
        first_t = sb("first_t", [P, COLS])
        samp_i = sb("samp_i", [P, T, BLOCK], I32)
        samp = sb("samp", [P, T])
        bidx_f = sb("bidx_f", [P, COLS])
        bidx = sb("bidx", [P, COLS], I32)
        assert NBLK == P * T

        node_table = nc.dram_tensor("node_table", [N, NW], F32).ap()
        h_table = nc.dram_tensor("h_table", [N, D], F32).ap()
        a_table = nc.dram_tensor("a_table", [N, 1], F32).ap()
        x1_table = nc.dram_tensor("x1_table", [N, D], F32).ap()
        blocks = nc.dram_tensor("edge_blocks", [LASTB + 1, 3 * SLOTS], I32).ap()

        x_in_s = sem("x_loaded")
        w_in = sem("weights_loaded")
        samp_in = sem("samples_loaded")
        blocks_out = sem("edge_blocks_written")
        iotas = sem("iotas_ready")
        consts = sem("constants_ready")
        wide_ok = sem("wide_weights_ready")
        dchain = sem("vector_chain")
        caught_ok = sem("caught_counted")
        h_sb = sem("h_copied")
        agg_ok = sem("sums_over_edges_ready")
        cmp_ok = sem("comparisons_ready")
        cnt_ok = sem("block_counts_ready")
        bidx_ok = sem("block_indices_ready")
        fetch_in = sem("edges_fetched")
        prep_ok = sem("edge_arrays_ready")
        et_ps = sem("edge_transposes_ready")
        et_sb = sem("edge_transposes_copied")
        sum_ps = sem("caught_summed")
        flag_ok = sem("flag_ready")
        xt_ps = sem("x_transposed")
        xt_sv = sem("x_transposes_copied_by_vector")
        xt_sa = sem("x_transposes_copied_by_scalar")
        nb_ps = sem("node_products_ready")
        nb_sb = sem("node_products_copied")
        a_ps = sem("a_products_ready")
        a_sb = sem("a_copied")
        new_x = sem("features_ready")
        A_hot = sem("C_onehots_ready")
        A_bank = sem("C_banks_ready")
        A_ev = sem("C_banks_copied")
        B_s = [sem(f"scores_ready{l}") for l in range(L)]
        B_p = [sem(f"counted_scores_ready{l}") for l in range(L)]
        B_mm = [sem(f"attention_steps_done{l}") for l in range(L)]
        B_ev = [sem(f"sums_copied{l}") for l in range(L)]
        C_hot = sem("W_onehots_ready")
        C_key = sem("W_keys_ready")
        C_bank = sem("W_banks_ready")
        C_ev = sem("W_banks_copied")
        C_t = sem("W_transposes_ready")
        C_tev = sem("W_transposes_copied")
        C_o = sem("out_products_ready")
        C_add = sem("out_products_added")
        tab = sem("tables_written")
        x0_in = sem("input_reloaded")
        x1_out = sem("x1_written")
        x1_in = sem("x1_loaded")
        g_in = sem("general_edges_loaded")
        g_idx = [sem(f"g_indices{l}") for l in range(PASSES)]
        g_go = [sem(f"g_go{l}") for l in range(PASSES)]
        g_rows = [sem(f"g_rows{l}") for l in range(PASSES)]
        g_score = [sem(f"g_score{l}") for l in range(PASSES)]
        g_hot = [sem(f"g_hot{l}") for l in range(PASSES)]
        g_oh = [sem(f"g_onehot{l}") for l in range(PASSES)]
        g_msg = [sem(f"g_messages{l}") for l in range(PASSES)]
        g_used = [sem(f"g_chunks_done{l}") for l in range(PASSES)]
        g_chain = sem("g_vector_chain")
        pre_gelu = sem("pre_gelu_ready")
        gelu_ok = sem("gelu_ready")
        cen_ok = sem("centred_ready")
        sq_ok = sem("squares_ready")
        var_ok = sem("variance_ready")
        std_ok = sem("deviation_ready")
        out_ok = sem("out_written")

        block = ctx.enter_context(nc.Block())
        tiles = "(t p) d -> p t d"
        hl = "(p t) d -> p t d"
        LOADS = 16 * (9 * L + 2)
        NORMS = [[l] for l in range(L)] + [[L + 1]]
        NORMS[L - 1].append(L)
        g_steps = [0]

        def is_fast(eng):
            eng.wait_ge(flag_ok, 1)
            return eng.value_load(fast_i[0:1, 0:1], min_val=0, max_val=1)

        def groups_loop(eng, body):
            with eng.Fori(0, GROUPS // 2) as i:
                body(i * 2, 0)
                body(i * 2 + 1, 1)
            if GROUPS % 2:
                body(GROUPS - 1, (GROUPS - 1) % 2)

        def steps_loop(eng, l, body, before=None):
            for j in range(T // JT):
                if before:
                    before(j)
                body(j * T, j, 0, (j * T) % 2, True)
                with eng.Fori(0, T // 2) as i:
                    body(i * 2 + (j * T + 1), j, i * 2 + 1, (j * T + 1) % 2, False)
                    body(i * 2 + (j * T + 2), j, i * 2 + 2, (j * T + 2) % 2, False)

        LAST = COLS - 1
        LAST_G = GROUPS - 5 * LAST

        def columns_loop(eng, body):
            body(0, 0, 5, False)
            with eng.Fori(0, (LAST - 2) // 2) as i:
                body(i * 2 + 1, 1, 5, True)
                body(i * 2 + 2, 0, 5, True)
            for s in range(1 + 2 * ((LAST - 2) // 2), LAST):
                body(s, s % 2, 5, True)
            body(LAST, LAST % 2, LAST_G, True)

        T_UNITS = [range(0, BANKFULS), range(BANKFULS, 2 * BANKFULS), (), (), ()]
        O_UNITS = [(), (), range(0, 3), range(3, BANKFULS), ()]
        ADDS = [(), (), (), range(0, 3), range(3, BANKFULS)]

        def units(table, g, ng):
            return [u for k in range(g, 5 if g == ng - 1 else g + 1) for u in table[k]]

        def span(q):
            return range(q * PER_BANK, min(T, (q + 1) * PER_BANK))

        FREE_A, FREE_AEV = 4, 6
        FREE_B = 2
        FREE_C, FREE_CEV, FREE_T, FREE_TEV, FREE_O, FREE_ADD = 4, 3, 14, 2, 7, 7

        NBU = -(-T // 3)
        U_ALL = NBU + 2 * BANKFULS

        def general_loads(sp, l):
            if l == 0:
                sp.wait_ge(A_ev, 3 * GROUPS + FREE_AEV)
                sp.dma_start(src_i, src.rearrange("(p k) -> p k", k=K)).then_inc(g_in, 16)
                sp.dma_start(dst_i, dst.rearrange("(p k) -> p k", k=K)).then_inc(g_in, 16)
                sp.dma_start(wgt, edge_weight.rearrange("(p k) -> p k", k=K)).then_inc(g_in, 16)
            if l < L:
                sp.wait_ge(nb_sb, (NBU + BANKFULS) * (l + 1))
                sp.dma_start(node_table.rearrange(hl, t=T), NB).then_inc(tab, 16)
                sp.wait_ge(a_sb, BANKFULS * (l + 1))
                sp.dma_start(a_table.rearrange("(o n) d -> o (n d)", o=1), ab[0:1, 0:N]).then_inc(tab, 16)
            else:
                sp.wait_ge(h_sb, BANKFULS)
                sp.dma_start(h_table.rearrange(tiles, p=P), so[:]).then_inc(tab, 16)
            sp.wait_ge(tab, 32 * (l + 1) if l < L else 32 * L + 16)

        @block.sync
        def _(sp):
            sp.dma_start(samp_i[:], dst.rearrange("(p b e) -> p b e", b=T, e=BLOCK)).then_inc(samp_in, 16)
            for f, a in enumerate((src, dst, edge_weight.bitcast(I32))):
                over = bass.AP(a.tensor, 0, [[BLOCK, LASTB + 1], [1, SLOTS]])
                sp.dma_start(blocks[:, f * SLOTS:(f + 1) * SLOTS], over).then_inc(blocks_out, 16)

            fast = is_fast(sp)
            for l in range(PASSES):
                with sp.If(fast == 0):
                    general_loads(sp, l)
                if l == L - 1:
                    sp.wait_ge(agg_ok, l + 1)
                    sp.dma_start(x_in, x.rearrange(tiles, p=P)).then_inc(x0_in, 16)
                    sp.wait_ge(new_x, L)
                    sp.dma_start(x1_table.rearrange(tiles, p=P), xs[:]).then_inc(x1_out, 16)
                    sp.wait_ge(x1_out, 16)
                    sp.dma_start(tmp, x1_table.rearrange(hl, t=T)).then_inc(x1_in, 16)
            sp.wait_ge(new_x, PASSES)
            sp.dma_start(out.rearrange(hl, t=T), accum).then_inc(out_ok, 16)
            sp.wait_ge(out_ok, 16)
            sp.wait_ge(blocks_out, 48)

        @block.gpsimd
        def _(pool):
            nc.gpsimd.iota(small_i[:], pattern=[[1, D]], base=0, channel_multiplier=0).then_inc(iotas, 1)
            nc.gpsimd.iota(part_i[:], pattern=[[0, 1]], base=0, channel_multiplier=1).then_inc(iotas, 1)
            nc.gpsimd.iota(wins, pattern=[[1, COLS * P]], base=0, channel_multiplier=0, allow_small_or_imprecise_dtypes=True).then_inc(iotas, 1)
            nc.gpsimd.iota(win_i[:], pattern=[[WIN * P, COLS]], base=0, channel_multiplier=WIN).then_inc(iotas, 1)
            nc.gpsimd.iota(iota_rep[:], pattern=[[1, P], [0, GP]], base=0, channel_multiplier=0, allow_small_or_imprecise_dtypes=True).then_inc(iotas, 1)
            nc.gpsimd.memset(edgesT[:].rearrange("q a w -> q (a w)"), 0.0).then_inc(iotas, 1)
            pool.wait_ge(blocks_out, 48)
            pool.wait_ge(bidx_ok, 1)
            for c in range(COLS):
                pool.indirect_dma_start(fetched[:, c].rearrange("p f e -> p (f e)"), None, blocks,
                                        bass.IndirectOffsetOnAxis(bidx[:, c:c + 1], 0)).then_inc(fetch_in, 16)
            fast = is_fast(pool)
            for l in range(PASSES):
                with pool.If(fast == 0):
                    pool.wait_ge(tab, 32 * (l + 1) if l < L else 32 * L + 16)
                    with pool.Fori(0, K) as k:
                        pool.wait_ge(g_idx[l], k * 2 + 2)
                        pool.wait_ge(g_msg[l], k + 1)
                        pool.sem_inc(g_go[l], 1)
                        if l < L:
                            pool.indirect_dma_start(rows, None, node_table, bass.IndirectOffsetOnAxis(gidx, 0)).then_inc(g_rows[l], 16)
                            pool.indirect_dma_start(a_dst, None, a_table, bass.IndirectOffsetOnAxis(aidx, 0)).then_inc(g_rows[l], 16)
                        else:
                            pool.indirect_dma_start(rows[:, 0:D], None, h_table, bass.IndirectOffsetOnAxis(gidx, 0)).then_inc(g_rows[l], 16)

        def nb_row(r, c0, c1):
            if isinstance(r, int):
                return NB[:, r, c0:c1]
            return nb[0:P, 0:T * NW].rearrange("p (t d) -> p t d", d=NW)[:, bass.ds(r, 1), c0:c1].rearrange("p o d -> p (o d)")

        def h_row(t):
            if isinstance(t, int):
                return so[:, t, :]
            return so[:, bass.ds(t, 1), :].rearrange("p o d -> p (o d)")

        def attention_products(pe, l):
            pe.sem_inc(B_mm[l], FREE_B)

            def before(j):
                if j >= 2:
                    pe.wait_ge(B_ev[l], j - 1)

            def step(n, j, r, slot, first):
                pe.wait_ge(B_p[l], n + 1 + FREE_B)
                for k in range(JT):
                    last = pe.matmul(ps[0:P, 2 * (j % 2) + k // 3, (k % 3) * (D + 1):(k % 3 + 1) * (D + 1)],
                                     PR[slot][:, k * P:(k + 1) * P], nb_row(r, 0, D + 1),
                                     start=(first and k % 3 == 0), stop=False, skip_group_check=True)
                last.then_inc(B_mm[l], 1)

            steps_loop(pe, l, step, before)

        def last_products(pe):
            pe.sem_inc(C_bank, FREE_C)
            pe.sem_inc(C_t, FREE_T)
            pe.sem_inc(C_o, FREE_O)

            def build(G, slot):
                pe.wait_ge(C_hot, G + 1)
                for i, (w0, w1) in enumerate(SPLIT):
                    pe.wait_ge(C_ev, G * 3 + (i + 1))
                    for w in range(w0, w1):
                        for j in range(3):
                            last = pe.matmul(ps[0:P, i, (w - w0) * KEYS:(w - w0 + 1) * KEYS], HI[:, slot, :, w],
                                             KW[:, slot, j, :, w], start=(j == 0), stop=(j == 2))
                    last.then_inc(C_bank, 1)

            def turn(sp, par, u, evacs):
                k, q = u // BANKFULS, u % BANKFULS
                pe.wait_ge(C_ev, evacs)
                pe.wait_ge(C_tev, sp * 14 + (u + 1))
                for r in span(q):
                    last = pe.transpose(ps[0:P, 3 + u % 2, (r % PER_BANK) * P:(r % PER_BANK + 1) * P],
                                        W[par][:, r, k * P:(k + 1) * P], ident[:])
                last.then_inc(C_t, 1)

            def product(sp, q, ks, turned):
                pe.wait_ge(C_tev, turned)
                pe.wait_ge(C_add, sp * 7 + (FREE_ADD + max(0, q - 2)))
                for r in span(q):
                    for k in range(ks):
                        last = pe.matmul(ps[0:P, 5 + q % 3, (r % PER_BANK) * D:(r % PER_BANK + 1) * D], WT[k][:, r, :],
                                         h_row(sp * 2 + k), start=(k == 0), stop=(k == ks - 1))
                last.then_inc(C_o, 1)

            def column(s, par, ng, behind):
                for g in range(ng):
                    build(s * 5 + g, (par + g) % 2)
                    if behind:
                        for u in units(T_UNITS, g, ng):
                            turn(s - 1, 1 - par, u, s * 15 + FREE_CEV)
                        for q in units(O_UNITS, g, ng):
                            product(s - 1, q, 2, (s - 1) * 14 + (14 + FREE_TEV))

            columns_loop(pe, column)
            for q in range(BANKFULS):
                turn(LAST, LAST % 2, q, LAST * 15 + 3 * LAST_G + FREE_CEV)
            for q in range(BANKFULS):
                product(LAST, q, 1, LAST * 14 + 7 + FREE_TEV)

        def general_products(pe, l):
            def chunk(k, first):
                pe.wait_ge(g_oh[l], k + 1)
                pe.wait_ge(g_msg[l], k + 2)
                for t in range(T):
                    last = pe.matmul(ps[0:P, t // PER_BANK, (t % PER_BANK) * D:(t % PER_BANK + 1) * D], onehot[:, t, :], msg,
                                     start=(first and t % PER_BANK == 0), stop=False, skip_group_check=True)
                if l < L:
                    last = pe.matmul(ps[0:P, 7, 0:T], oh_row, oh_s, start=first, stop=False, skip_group_check=True)
                last.then_inc(g_used[l], 1)

            pe.sem_inc(g_used[l], 1)
            chunk(0, True)
            with pe.Fori(1, K) as k:
                chunk(k, False)

        @block.tensor
        def _(pe):
            pe.wait_ge(consts, 1)
            for b in range(T):
                pe.wait_ge(cmp_ok, b + 1)
                for c in range(COLS):
                    last = pe.matmul(ps[0:P, 7, c:c + 1], cmp_[:, b, c * P:(c + 1) * P], ones16[:],
                                     start=(b == 0 and c == 0), stop=False, skip_group_check=True)
            last.then_inc(cnt_ok, 1)

            def nodes(l):
                pe.wait_ge(x_in_s, 16)
                pe.wait_ge(consts, 2)
                if l:
                    pe.wait_ge(new_x, l)
                for q in range(BANKFULS):
                    for t in span(q):
                        last = pe.transpose(ps[:, q, (t % PER_BANK) * P:(t % PER_BANK + 1) * P], xs[:, t, :], ident[:])
                    last.then_inc(xt_ps, 1)
                pe.wait_ge(xt_sv, 4 * (l + 1))
                pe.wait_ge(xt_sa, 3 * (l + 1))
                pe.wait_ge(w_in, LOADS)
                if l == L:
                    for q in range(BANKFULS):
                        for t in span(q):
                            last = pe.matmul(ps[0:P, q, (t % PER_BANK) * D:(t % PER_BANK + 1) * D],
                                             xT[:, t * P:(t + 1) * P], kern[:], start=True, stop=True)
                        last.then_inc(nb_ps, 1)
                    return
                pe.wait_ge(wide_ok, L)
                for u in range(U_ALL):
                    if u >= 7:
                        pe.wait_ge(nb_sb, (NBU + BANKFULS) * l + u - 6)
                    if u < NBU:
                        for r in range(3 * u, min(T, 3 * u + 3)):
                            last = pe.matmul(ps[0:P, u % 7, (r % 3) * NW:(r % 3 + 1) * NW], xT[:, r::T], wideN[:, l, :], start=True, stop=True)
                        last.then_inc(nb_ps, 1)
                    elif u < NBU + BANKFULS:
                        for t in span(u - NBU):
                            last = pe.matmul(ps[0:P, u % 7, (t % PER_BANK) * D:(t % PER_BANK + 1) * D], xT[:, t * P:(t + 1) * P],
                                             wideS[:, l, :], start=True, stop=True)
                        last.then_inc(nb_ps, 1)
                    else:
                        q = u - NBU - BANKFULS
                        n = len(span(q)) * P
                        pe.matmul(ps[0:P, u % 7, 0:n], wa1_rep[:, l, :], xT[:, q * PER_BANK * P:q * PER_BANK * P + n],
                                  start=True, stop=True).then_inc(a_ps, 1)

            nodes(0)

            pe.wait_ge(nb_sb, NBU + BANKFULS)
            pe.wait_ge(a_sb, BANKFULS)
            for u in range(10):
                a, half = u // 2, u % 2
                pe.wait_ge(prep_ok, a + 1)
                if u >= 7:
                    pe.wait_ge(et_sb, u - 6)
                cs = range(8) if half == 0 else range(8, COLS)
                for j, c in enumerate(cs):
                    last = pe.transpose(ps[:, u % 7, :].bitcast(BF16)[:, j * 128:j * 128 + P], e_16[a][:, c, :], ident16[:])
                last.then_inc(et_ps, 1)
            pe.wait_ge(caught_ok, 1)
            pe.wait_ge(bidx_ok, 1)
            pe.matmul(ps[0:1, 7, 0:1], caught[:], ones[:], start=True, stop=True).then_inc(sum_ps, 1)

            pe.wait_ge(et_sb, 10)
            pe.sem_inc(A_bank, FREE_A)

            def count_group(G, slot):
                pe.wait_ge(A_hot, G + 1)
                for i, (w0, w1) in enumerate(SPLIT):
                    pe.wait_ge(A_ev, G * 3 + (i + 1))
                    for w in range(w0, w1):
                        last = pe.matmul(ps[0:P, 3 * slot + i, (w - w0) * KEYS:(w - w0 + 1) * KEYS], HI[:, slot, :, w],
                                         KEY[:, slot, :, w], start=True, stop=True)
                    last.then_inc(A_bank, 1)

            groups_loop(pe, count_group)
            pe.wait_ge(A_ev, 3 * GROUPS + FREE_AEV)

            fast = is_fast(pe)
            for l in range(PASSES):
                if l:
                    nodes(l)
                if l < L:
                    pe.wait_ge(nb_sb, (NBU + BANKFULS) * (l + 1))
                    pe.wait_ge(a_sb, BANKFULS * (l + 1))
                else:
                    pe.wait_ge(h_sb, BANKFULS)
                with pe.If(fast == 1):
                    if l < L:
                        attention_products(pe, l)
                    else:
                        last_products(pe)
                with pe.If(fast == 0):
                    general_products(pe, l)

        def attention_scores(act, l):
            def step(n, j, r, slot, first):
                act.wait_ge(B_p[l], n + 1)
                nc.scalar.activation(S[slot], ab[:, j * JC:(j + 1) * JC], ACT.Sigmoid, bias=nb_row(r, B, B + 1)).then_inc(B_s[l], 1)

            act.wait_ge(nb_sb, (NBU + BANKFULS) * (l + 1))
            act.wait_ge(a_sb, BANKFULS * (l + 1))
            if l == 0:
                act.wait_ge(A_bank, 3 * GROUPS + FREE_A)
            steps_loop(act, l, step)

        def last_copies(act):
            act.sem_inc(C_ev, FREE_CEV)
            act.sem_inc(C_tev, FREE_TEV)
            act.wait_ge(agg_ok, L)

            def build(G, g, par, s):
                for i, (w0, w1) in enumerate(SPLIT):
                    act.wait_ge(C_bank, G * 3 + (i + 1 + FREE_C))
                    n = (w1 - w0) * WIN
                    c0 = g * GC + WIN * w0
                    nc.scalar.copy(W[par][:, :, c0:c0 + n], ps[0:P, i, 0:n * T].rearrange("p (c r) -> p r c", r=T)).then_inc(C_ev, 1)

            def turn(sp, u):
                k, q = u // BANKFULS, u % BANKFULS
                act.wait_ge(C_t, sp * 14 + (u + 1 + FREE_T))
                act.wait_ge(C_o, sp * 7 + FREE_O)
                n = len(span(q))
                nc.scalar.copy(WT[k][:, q * PER_BANK:q * PER_BANK + n, :],
                               ps[0:P, 3 + u % 2, 0:n * P].rearrange("p (r c) -> p r c", c=P)).then_inc(C_tev, 1)

            def column(s, par, ng, behind):
                if behind:
                    act.wait_ge(C_t, s * 14)
                for g in range(ng):
                    build(s * 5 + g, g, par, s)
                    if behind:
                        for u in units(T_UNITS, g, ng):
                            turn(s - 1, u)

            columns_loop(act, column)
            for q in range(BANKFULS):
                turn(LAST, q)

        @block.scalar
        def _(act):
            act.dma_start(xs[:], x.rearrange(tiles, p=P)).then_inc(x_in_s, 16)
            for l in range(L):
                act.dma_start(wideN[:, l, 0:D], Wn[l]).then_inc(w_in, 16)
                act.dma_start(wideS[:, l, :], Ws[l]).then_inc(w_in, 16)
                act.dma_start(wa1[:, l:l + 1], Wa[l, 0:D].unsqueeze(1)).then_inc(w_in, 16)
                act.dma_start(wa2[:, l, :], Wa[l, D:2 * D].partition_broadcast(D)).then_inc(w_in, 16)
                act.dma_start(biasN[:, l, 0:D], bn[l].partition_broadcast(P)).then_inc(w_in, 16)
                act.dma_start(biasS[:, l, :], bs[l].partition_broadcast(P)).then_inc(w_in, 16)
                act.dma_start(ba_b[:, l:l + 1], ba[l:l + 1].partition_broadcast(P)).then_inc(w_in, 16)
                act.dma_start(gam[:, l, :], gamma[l].partition_broadcast(P)).then_inc(w_in, 16)
                act.dma_start(bet[:, l, :], beta[l].partition_broadcast(P)).then_inc(w_in, 16)
            act.dma_start(kern[:], kernel1).then_inc(w_in, 16)
            act.dma_start(bi1[:], bias1.partition_broadcast(P)).then_inc(w_in, 16)

            def nodes(l):
                for q in range(1, BANKFULS, 2):
                    n = len(span(q)) * P
                    act.wait_ge(xt_ps, l * BANKFULS + q + 1)
                    nc.scalar.copy(xT[:, q * PER_BANK * P:q * PER_BANK * P + n], ps[:, q, 0:n]).then_inc(xt_sa, 1)
                if l == L:
                    for q in range(BANKFULS):
                        t = span(q)
                        act.wait_ge(nb_ps, (NBU + BANKFULS) * L + q + 1)
                        nc.scalar.copy(so[:, t.start:t.stop, :], ps[0:P, q, 0:len(t) * D].rearrange("p (t d) -> p t d", d=D)).then_inc(h_sb, 1)
                    return
                act.wait_ge(w_in, LOADS)
                act.wait_ge(cmp_ok, T)
                for q in range(BANKFULS):
                    n = len(span(q)) * P
                    act.wait_ge(a_ps, l * BANKFULS + q + 1)
                    nc.scalar.activation(ab[:, q * PER_BANK * P:q * PER_BANK * P + n], ps[0:P, (q + NBU + BANKFULS) % 7, 0:n], ACT.Identity,
                                         bias=ba_b[:, l:l + 1]).then_inc(a_sb, 1)

            nodes(0)
            act.wait_ge(iotas, 6)
            for u in range(10):
                a, half = u // 2, u % 2
                c0, c1 = (0, 8) if half == 0 else (8, COLS)
                act.wait_ge(et_ps, u + 1)
                nc.scalar.copy(edgesT[:, a, c0 * 5 * GP:c1 * 5 * GP].rearrange("q (c g w) -> q c g w", g=5, w=GP)[:, :, :, 0:GW],
                               ps[:, u % 7, :].bitcast(BF16)[:, 0:(c1 - c0) * 128].rearrange("q (c w) -> q c w", w=128)[:, :, 0:P]
                               .rearrange("q c (g w) -> q c g w", w=GW)).then_inc(et_sb, 1)
            act.sem_inc(A_ev, FREE_AEV)
            act.wait_ge(prep_ok, 5)

            def count_copies(G, slot):
                for i, (w0, w1) in enumerate(SPLIT):
                    act.wait_ge(A_bank, G * 3 + (i + 1 + FREE_A))
                    n = (w1 - w0) * WIN
                    nc.scalar.copy(C[:, :, bass.ds(G * GC + WIN * w0, n)],
                                   ps[0:P, 3 * slot + i, 0:n * T].rearrange("p (c r) -> p r c", r=T)).then_inc(A_ev, 1)

            groups_loop(act, count_copies)

            fast = is_fast(act)
            for l in range(PASSES):
                if l:
                    nodes(l)
                with act.If(fast == 1):
                    if l < L:
                        attention_scores(act, l)
                    else:
                        last_copies(act)
                if l < L:
                    with act.If(fast == 0):
                        with act.Fori(0, K) as k:
                            act.wait_ge(g_rows[l], k * 32 + 32)
                            nc.scalar.activation(score, rows[:, B:B + 1], ACT.Sigmoid, bias=a_dst).then_inc(g_score[l], 1)
                    act.wait_ge(pre_gelu, l + 1)
                    nc.scalar.activation(tmp, tmp, ACT.Gelu).then_inc(gelu_ok, 1)
                for i in NORMS[l]:
                    act.wait_ge(cen_ok, i + 1)
                    if l < L:
                        nc.scalar.activation(accum, xs[:], ACT.Square).then_inc(sq_ok, 1)
                    else:
                        nc.scalar.activation(xs[:], accum, ACT.Square).then_inc(sq_ok, 1)
                    act.wait_ge(var_ok, i + 1)
                    nc.scalar.activation(st[:, 2, :], st[:, 1, :], ACT.Sqrt).then_inc(std_ok, 1)

        def attention_weights(dve, l):
            dve.sem_inc(B_p[l], FREE_B)

            def copy_sums(j):
                dve.wait_ge(B_mm[l], (j + 1) * T + FREE_B)
                nc.vector.tensor_copy(agg[:, j * JT:j * JT + 3, :], ps[0:P, 2 * (j % 2), 0:3 * (D + 1)].rearrange("p (t d) -> p t d", d=D + 1))
                nc.vector.tensor_copy(agg[:, j * JT + 3:j * JT + 5, :], ps[0:P, 2 * (j % 2) + 1, 0:2 * (D + 1)]
                                      .rearrange("p (t d) -> p t d", d=D + 1)).then_inc(B_ev[l], 1)

            def before(j):
                if j:
                    copy_sums(j - 1)

            def step(n, j, r, slot, first):
                dve.wait_ge(B_s[l], n + 1)
                dve.wait_ge(B_mm[l], n + 1)
                c = C[:, r, j * JC:(j + 1) * JC] if isinstance(r, int) else C[:, bass.ds(r, 1), j * JC:(j + 1) * JC].rearrange("p o c -> p (o c)")
                nc.vector.tensor_tensor(PR[slot], S[slot], c, ALU.mult).then_inc(B_p[l], 1)

            steps_loop(dve, l, step, before)
            copy_sums(T // JT - 1)
            dve.wait_ge(B_ev[l], T // JT)

        def last_onehots(dve, gathered):
            dve.sem_inc(C_add, FREE_ADD)

            def build(G, slot):
                dve.wait_ge(C_bank, G * 3 + 1)
                nc.vector.tensor_tensor(KEY[:, slot], gathered(1, G).to_broadcast([128, KEYS, GP]), iota_rep[:, 0:KEYS, :],
                                        ALU.is_equal).then_inc(C_key, 1)
                nc.vector.tensor_tensor(HI[:, slot], gathered(0, G).to_broadcast([128, P, GP]), iota_rep[:], ALU.is_equal)
                dve.wait_ge(C_key, G + 1)
                for j in range(3):
                    last = nc.vector.tensor_tensor(KW[:, slot, j], KEY[:, slot], gathered(2 + j, G).to_broadcast([128, KEYS, GP]), ALU.mult)
                last.then_inc(C_hot, 1)

            def add(sp, q):
                t = span(q)
                dve.wait_ge(C_o, sp * 7 + (q + 1 + FREE_O))
                dve.wait_ge(C_add, sp * 7 + (q + 1))
                nc.vector.tensor_tensor(accum[:, t.start:t.stop, :], accum[:, t.start:t.stop, :],
                                        ps[0:P, 5 + q % 3, 0:len(t) * D].rearrange("p (t d) -> p t d", d=D), ALU.add).then_inc(C_add, 1)

            def column(s, par, ng, behind):
                for g in range(ng):
                    build(s * 5 + g, (par + g) % 2)
                    if behind:
                        for q in units(ADDS, g, ng):
                            add(s - 1, q)

            columns_loop(dve, column)
            for q in range(BANKFULS):
                add(LAST, q)
            dve.wait_ge(C_add, 7 * (LAST + 1) + FREE_ADD)

        def general_sums(dve, l):

            def link(ins):
                ins.then_inc(g_chain, 1)
                g_steps[0] += 1
                dve.wait_ge(g_chain, g_steps[0])

            if l == 0:
                dve.wait_ge(g_in, 48)
                for ids, parts, m in ((src_i, src_hl, T), (dst_i, dst_tl, P)):
                    link(nc.vector.tensor_copy(parts[:, 1, :], ids))
                    link(nc.vector.tensor_scalar(parts[:, 0, :], parts[:, 1, :], -(m - 1) / 2, 1.0 / m, ALU.add, ALU.mult))
                    link(nc.vector.tensor_scalar(parts[:, 0, :], parts[:, 0, :], ROUND, -ROUND, ALU.add, ALU.add))
                    link(nc.vector.scalar_tensor_tensor(parts[:, 1, :], parts[:, 0, :], -float(m), parts[:, 1, :], ALU.mult, ALU.add))
            dve.sem_inc(g_msg[l], 1)
            g_i = src_i if l < L else dst_i
            row, blk = (dst_tl[:, 1, :], dst_tl[:, 0, :]) if l < L else (src_hl[:, 0, :], src_hl[:, 1, :])
            with dve.Fori(0, K) as k:
                nc.vector.tensor_copy(gidx, g_i[:, bass.ds(k, 1)]).then_inc(g_idx[l], 1)
                nc.vector.tensor_copy(aidx, dst_i[:, bass.ds(k, 1)]).then_inc(g_idx[l], 1)
                dve.wait_ge(g_used[l], k + 1)
                nc.vector.tensor_scalar(oh_row, iota_f[:, 0:P], row[:, bass.ds(k, 1)], None, ALU.is_equal).then_inc(g_hot[l], 1)
                nc.vector.tensor_scalar(oh_blk, iota_f[:, 0:T], blk[:, bass.ds(k, 1)], None, ALU.is_equal).then_inc(g_hot[l], 1)
                dve.wait_ge(g_hot[l], k * 2 + 2)
                nc.vector.tensor_tensor(onehot, oh_row.unsqueeze(1).to_broadcast([P, T, P]), oh_blk.unsqueeze(2).to_broadcast([P, T, P]),
                                        ALU.mult).then_inc(g_oh[l], 1)
                if l < L:
                    dve.wait_ge(g_score[l], k + 1)
                    nc.vector.tensor_scalar(oh_s, oh_blk, score, None, ALU.mult)
                    nc.vector.tensor_scalar(msg, rows[:, 0:D], score, None, ALU.mult).then_inc(g_msg[l], 1)
                else:
                    dve.wait_ge(g_rows[l], k * 16 + 16)
                    nc.vector.tensor_scalar(msg, rows[:, 0:D], wgt[:, bass.ds(k, 1)], None, ALU.mult).then_inc(g_msg[l], 1)
            dve.wait_ge(g_used[l], K + 1)
            for q in range(BANKFULS):
                t = span(q)
                target = agg[:, t.start:t.stop, 0:D] if l < L else accum[:, t.start:t.stop, :]
                link(nc.vector.tensor_copy(target, ps[0:P, q, 0:len(t) * D].rearrange("p (t d) -> p t d", d=D)))
            if l < L:
                link(nc.vector.tensor_copy(agg[:, :, D], ps[0:P, 7, 0:T]))

        @block.vector
        def _(dve):
            steps = [0]

            def link(ins):
                ins.then_inc(dchain, 1)
                steps[0] += 1
                dve.wait_ge(dchain, steps[0])

            def spread(v):
                return v.unsqueeze(2).to_broadcast([P, T, D])

            def along(v):
                return v.unsqueeze(1).to_broadcast([P, T, D])

            dve.wait_ge(iotas, 6)
            dve.wait_ge(samp_in, 16)
            link(nc.vector.tensor_scalar(samp[:], samp_i[:, :, 0], 1.0 / WIN, None, ALU.mult))
            nc.vector.memset(ones16[:], 1.0).then_inc(consts, 1)
            for b in range(T):
                nc.vector.tensor_scalar(cmp_[:, b, :], wins, samp[:, b:b + 1], None, ALU.is_gt).then_inc(cmp_ok, 1)
            link(nc.vector.memset(ones[:], 1.0))
            link(nc.vector.tensor_copy(iota_f[:], small_i[0:P, :]))
            link(nc.vector.tensor_copy(part[:], part_i[:]))
            link(nc.vector.tensor_copy(first_t[:], win_i[:]))
            link(nc.vector.tensor_scalar(ident[:], iota_f[:, 0:P], part[:], None, ALU.is_equal))
            link(nc.vector.tensor_copy(ident16[:], ident[:]))
            dve.sem_inc(consts, 1)
            dve.wait_ge(cnt_ok, 1)
            link(nc.vector.tensor_scalar(bidx_f[:], ps[0:P, 7, 0:COLS], -1.0, 0.0, ALU.add, ALU.max))
            nc.vector.tensor_scalar(bidx[:], bidx_f[:], float(LASTB), None, ALU.min).then_inc(bidx_ok, 1)
            dve.wait_ge(w_in, LOADS)
            for l in range(L):
                link(nc.vector.tensor_tensor_reduce(prod[:], wideN[:, l, 0:D], wa2[:, l, :], 1.0, 0.0, ALU.mult, ALU.add, wideN[:, l, B:B + 1]))
                link(nc.vector.tensor_tensor_reduce(prod[0:P], biasN[:, l, 0:D], wa2[0:P, l, :], 1.0, 0.0, ALU.mult, ALU.add, biasN[:, l, B:B + 1]))
                link(nc.vector.memset(wideN[:, l, ONE:ONE + 1], 0.0))
                link(nc.vector.memset(biasN[:, l, ONE:ONE + 1], 1.0))
                link(nc.vector.memset(wa1_rep[:, l, :], 1.0))
                nc.vector.tensor_scalar(wa1_rep[:, l, :], wa1_rep[:, l, :], wa1[:, l:l + 1], None, ALU.mult).then_inc(wide_ok, 1)

            def nodes(l):
                for q in range(0, BANKFULS, 2):
                    n = len(span(q)) * P
                    dve.wait_ge(xt_ps, l * BANKFULS + q + 1)
                    nc.vector.tensor_copy(xT[:, q * PER_BANK * P:q * PER_BANK * P + n], ps[:, q, 0:n]).then_inc(xt_sv, 1)
                if l == L:
                    return
                for u in range(NBU):
                    n = min(3, T - 3 * u)
                    dve.wait_ge(nb_ps, l * (NBU + BANKFULS) + u + 1)
                    nc.vector.tensor_tensor(NB[:, 3 * u:3 * u + n, :], ps[0:P, u % 7, 0:n * NW].rearrange("p (t d) -> p t d", d=NW),
                                            biasN[:, l, :].unsqueeze(1).to_broadcast([P, n, NW]), ALU.add).then_inc(nb_sb, 1)
                for q in range(BANKFULS):
                    u, t = NBU + q, span(q)
                    dve.wait_ge(nb_ps, l * (NBU + BANKFULS) + u + 1)
                    nc.vector.tensor_tensor(so[:, t.start:t.stop, :], ps[0:P, u % 7, 0:len(t) * D].rearrange("p (t d) -> p t d", d=D),
                                            biasS[:, l, :].unsqueeze(1).to_broadcast([P, len(t), D]), ALU.add).then_inc(nb_sb, 1)

            nodes(0)

            f0, f1, f2, f3 = e_f
            dve.wait_ge(fetch_in, 16 * COLS)
            link(nc.vector.tensor_copy(f0, fetched[:, :, 0, :]))
            link(nc.vector.tensor_scalar(f1, f0, -(T - 1) / 2, 1.0 / T, ALU.add, ALU.mult))
            link(nc.vector.tensor_scalar(f1, f1, ROUND, -ROUND, ALU.add, ALU.add))
            nc.vector.tensor_copy(e_16[0], f1).then_inc(prep_ok, 1)
            link(nc.vector.scalar_tensor_tensor(f0, f1, -float(T), f0, ALU.mult, ALU.add))
            link(nc.vector.tensor_copy(f2, fetched[:, :, 1, :]))
            link(nc.vector.tensor_tensor(f2, f2, first_t[:].unsqueeze(2).to_broadcast([P, COLS, SLOTS]), ALU.subtract))
            nc.vector.scalar_tensor_tensor(e_16[1], f2, float(T), f0, ALU.mult, ALU.add).then_inc(prep_ok, 1)
            link(nc.vector.tensor_scalar(f3, f2, -(WIN - 1) / 2, None, ALU.add))
            link(nc.vector.tensor_tensor(f3, f3, f3, ALU.mult))
            nc.vector.tensor_scalar(f0, f3, WIN * WIN / 4, 0.0, ALU.is_lt, ALU.add, accum_out=caught[:]).then_inc(caught_ok, 1)
            w = fetched[:, :, 2, :].bitcast(F32)
            dve.wait_ge(prep_ok, 2)
            nc.vector.tensor_copy(e_16[2], w).then_inc(prep_ok, 1)
            dve.wait_ge(prep_ok, 3)
            link(nc.vector.tensor_tensor(f1, w, e_16[2], ALU.subtract))
            nc.vector.tensor_copy(e_16[3], f1).then_inc(prep_ok, 1)
            dve.wait_ge(prep_ok, 4)
            link(nc.vector.tensor_tensor(f2, f1, e_16[3], ALU.subtract))
            nc.vector.tensor_copy(e_16[4], f2).then_inc(prep_ok, 1)
            dve.wait_ge(sum_ps, 1)
            nc.vector.tensor_scalar(fast_i[:], ps[0:1, 7, 0:1], float(all_edges), None, ALU.is_equal).then_inc(flag_ok, 1)

            def gathered(a, G):
                return edgesT[:, a, bass.ds(G * GP, GP)].unsqueeze(1)

            dve.wait_ge(et_sb, 10)

            def count_onehots(G, slot):
                dve.wait_ge(A_bank, G * 3 + 1)
                nc.vector.tensor_tensor(HI[:, slot], gathered(0, G).to_broadcast([128, P, GP]), iota_rep[:], ALU.is_equal)
                nc.vector.tensor_tensor(KEY[:, slot], gathered(1, G).to_broadcast([128, KEYS, GP]), iota_rep[:, 0:KEYS, :],
                                        ALU.is_equal).then_inc(A_hot, 1)

            groups_loop(dve, count_onehots)

            fast = is_fast(dve)
            for l in range(PASSES):
                if l:
                    nodes(l)
                if l == L:
                    dve.wait_ge(h_sb, BANKFULS)
                    link(nc.vector.memset(accum, 0.0))
                with dve.If(fast == 1):
                    if l < L:
                        attention_weights(dve, l)
                    else:
                        last_onehots(dve, gathered)
                with dve.If(fast == 0):
                    general_sums(dve, l)
                dve.sem_inc(agg_ok, 1)
                if l < L:
                    link(nc.vector.tensor_scalar(st[:, 0, :], agg[:, :, D], EPS_SCORE, None, ALU.add))
                    link(nc.vector.reciprocal(st[:, 0, :], st[:, 0, :]))
                    link(nc.vector.tensor_tensor(tmp, agg[:, :, 0:D], spread(st[:, 0, :]), ALU.mult))
                    link(nc.vector.tensor_tensor(tmp, tmp, so[:], ALU.add))
                    dve.sem_inc(pre_gelu, 1)
                    dve.wait_ge(gelu_ok, l + 1)
                    link(nc.vector.tensor_tensor(xs[:], xs[:], tmp, ALU.add))
                    y, norms = xs[:], NORMS[l]
                else:
                    dve.wait_ge(x1_in, 16)
                    link(nc.vector.tensor_tensor(accum, accum, along(bi1[:]), ALU.add))
                    link(nc.vector.scalar_tensor_tensor(accum, accum, 0.0, tmp, ALU.max, ALU.add))
                    y, norms = accum, NORMS[l]
                for i in norms:
                    if l == L - 1 and i == norms[-1]:
                        dve.wait_ge(x0_in, 16)
                        link(nc.vector.tensor_tensor(y, y, x_in, ALU.add))
                    link(nc.vector.tensor_reduce(st[:, 0, :], y, AX.X, ALU.add))
                    link(nc.vector.tensor_scalar(st[:, 0, :], st[:, 0, :], -1.0 / D, None, ALU.mult))
                    nc.vector.tensor_tensor(y, y, spread(st[:, 0, :]), ALU.add).then_inc(cen_ok, 1)
                    dve.wait_ge(sq_ok, i + 1)
                    link(nc.vector.tensor_reduce(st[:, 1, :], accum if l < L else xs[:], AX.X, ALU.add))
                    link(nc.vector.tensor_scalar(st[:, 1, :], st[:, 1, :], 1.0 / D, EPS_NORM, ALU.mult, ALU.add))
                    dve.sem_inc(var_ok, 1)
                    dve.wait_ge(std_ok, i + 1)
                    link(nc.vector.reciprocal(st[:, 0, :], st[:, 2, :]))
                    link(nc.vector.tensor_tensor(y, y, spread(st[:, 0, :]), ALU.mult))
                    if l < L and i == norms[0]:
                        link(nc.vector.tensor_tensor(y, y, along(gam[:, l, :]), ALU.mult))
                        link(nc.vector.tensor_tensor(y, y, along(bet[:, l, :]), ALU.add))
                dve.sem_inc(new_x, 1)


_INS = ['x', 'src', 'dst', 'edge_weight', 'L0_gnn_Ws', 'L0_gnn_bs', 'L0_gnn_Wn', 'L0_gnn_bn', 'L0_gnn_Wa', 'L0_gnn_ba',
        'L0_gnn_gamma', 'L0_gnn_beta', 'L1_gnn_kernel', 'L1_gnn_bias']


def kernel(**inputs):
    import numpy as _np
    import concourse.bacc as _bacc
    from concourse import mybir as _mybir
    from concourse.bass_utils import run_bass_kernel_spmd as _run

    nc = _bacc.Bacc("TRN2", target_bir_lowering=False, num_devices=1)
    arrays, args = {}, []
    for name in _INS:
        a = _np.ascontiguousarray(inputs[name])
        arrays[f"in_{name}_dram"] = a
        args.append(nc.dram_tensor(f"in_{name}_dram", a.shape, _mybir.dt.from_np(a.dtype), kind="ExternalInput").ap())
    out = nc.dram_tensor("out_dram", (3125, 128), _mybir.dt.float32, kind="ExternalOutput").ap()
    gnn_kernel(nc, *args, out)
    r = _run(nc, [arrays], core_ids=[0])
    return r.results[0]["out_dram"]
```

```python
from contextlib import ExitStack

import concourse.bass as bass
from concourse import mybir

ALU = mybir.AluOpType
ACT = mybir.ActivationFunctionType
AX = mybir.AxisListType
F32 = mybir.dt.float32
F16 = mybir.dt.float16
BF16 = mybir.dt.bfloat16
I32 = mybir.dt.int32
U8 = mybir.dt.uint8

EPS_NORM = 1e-5
EPS_SCORE = 1e-6
ROUND = float(3 << 22)



def gnn_kernel(nc, x, src, dst, edge_weight, Ws, bs, Wn, bn, Wa, ba, gamma, beta, kernel1, bias1, out):
    N, D = x.shape
    E = src.shape[0]
    L = Ws.shape[0]
    P = 125
    T = N // P
    K = E // P
    assert N == P * T and E == P * K and D == 128
    PASSES = L + 1

    PER_BANK = 4
    BANKFULS = -(-T // PER_BANK)
    NW = D + 2
    ONE, B = D, D + 1

    WIN = 2
    GW = 25
    GP = 26
    KEYS = WIN * T
    COLS = -(-N // (WIN * P))
    GROUPS = -(-N // (WIN * GW))
    SLOTS = 128
    HV = 128
    BLOCK = 32
    NBLK = E // BLOCK
    LASTB = (E - SLOTS) // BLOCK
    SPLIT = [(0, 9), (9, 17), (17, 25)]
    CW = COLS * P * WIN
    GC = GW * WIN
    JT = 5
    JC = JT * P
    READY = [-(-(j + 1) * JC // GC) for j in range(T // JT)]

    with ExitStack() as ctx:
        def sb(name, shape, dt=F32):
            return ctx.enter_context(nc.sbuf_tensor(name, shape, dt))

        def sem(name):
            return ctx.enter_context(nc.semaphore(name))

        ps = ctx.enter_context(nc.psum_tensor("ps", [128, 8, 512], F32))

        xs = sb("xs", [P, T, D])
        xa = sb("xa", [128, T * D])
        nb = sb("nb", [128, 4056])
        so = sb("so", [P, T, D])
        ab = sb("ab", [P, T * D])
        edgesT = sb("edgesT", [128, 5, COLS * 5 * GP], BF16)
        hot = sb("hot", [128, 2, HV + KEYS, GP], BF16)
        iota_rep = sb("iota_rep", [128, HV, GP], BF16)
        arena = sb("arena", [128, 20352])
        wideN = sb("wideN", [D, L, NW])
        wideS = sb("wideS", [D, L, D])
        wa1 = sb("wa1", [D, L])
        wa1_rep = sb("wa1_rep", [D, L, P])
        kern = sb("kern", [D, D])
        biasN = sb("biasN", [P, L, NW])
        biasS = sb("biasS", [P, L, D])
        ba_b = sb("ba_b", [P, L])
        gam = sb("gam", [P, L, D])
        bet = sb("bet", [P, L, D])
        bi1 = sb("bi1", [P, D])
        den = sb("den", [P, T])
        stats = sb("stats", [P, JT, 6])
        mv = sb("mv", [P, 2, JT, 2])
        veps = sb("veps", [P, 2, JT])
        rstd = sb("rstd", [P, 2, JT])
        minus_half = sb("minus_half", [P, JT])
        ident = sb("ident", [128, 128])
        ident16 = sb("ident16", [128, 128], BF16)
        ones = sb("ones", [P, 1])
        ones16 = sb("ones16", [P, 1], BF16)
        hcur = sb("hcur", [P, 2, 2, D])
        part = sb("part", [128, 1])
        caught = sb("caught", [P, 1])
        fast_i = sb("fast_i", [1, 1], I32)

        xT = xa[:, 0:N]
        accum = xa[0:P, 0:T * D].rearrange("p (t d) -> p t d", d=D)
        NB = nb[0:P, 0:T * NW].rearrange("p (t d) -> p t d", d=NW)
        accT = xa[:, 0:N]
        KW = nb[:, 0:3 * KEYS * GP].bitcast(BF16).rearrange("q (s k j w) -> q s k j w", s=2, j=3, w=GP)
        tmp = ab[:].rearrange("p (t d) -> p t d", d=D)
        HI = hot[:, :, 0:HV, :]
        KEY = hot[:, :, HV:HV + KEYS, :]
        hotf = hot[:].rearrange("q s v w -> q (s v w)").bitcast(F32)
        x_in = hotf[0:P, 0:T * D].rearrange("p (t d) -> p t d", d=D)
        score_bufs = sb("score_bufs", [P, 3 * JC])
        S = [score_bufs[:, j * JC:(j + 1) * JC] for j in range(2)]
        PR = [score_bufs[:, 2 * JC:3 * JC], nb[0:P, T * NW:T * NW + JC]]

        flat = arena[:]

        class Carve:
            def __init__(self):
                self.at = 0

            def __call__(self, parts, n):
                self.at += n
                assert self.at <= 20352
                return flat[0:parts, self.at - n:self.at]

        cmp_ = flat[0:P, 0:T * COLS * P // 2 + 1].bitcast(BF16)[:, 0:T * COLS * P].rearrange("p (b w) -> p b w", b=T)
        cut = Carve()
        fetched = cut(P, COLS * 3 * SLOTS).bitcast(I32).rearrange("p (c f e) -> p c f e", c=COLS, f=3)
        e_f = [cut(P, COLS * SLOTS).rearrange("p (c e) -> p c e", c=COLS) for _ in range(6)]
        e_16 = [cut(P, COLS * SLOTS // 2).bitcast(BF16).rearrange("p (c e) -> p c e", c=COLS) for _ in range(5)]
        C = flat[0:P, 0:-(-T * CW // 4)].bitcast(U8)[:, 0:T * CW].rearrange("p (r c) -> p r c", r=T)
        cut = Carve()
        W = [cut(P, T * 2 * P).rearrange("p (r c) -> p r c", r=T) for _ in range(2)]
        WT = [cut(P, T * P).rearrange("p (r q) -> p r q", r=T) for _ in range(2)]
        cut = Carve()
        src_i = cut(P, K).bitcast(I32)
        dst_i = cut(P, K).bitcast(I32)
        wgt = cut(P, K)
        src_hl = cut(P, 2 * K).rearrange("p (j k) -> p j k", j=2)
        dst_tl = cut(P, 2 * K).rearrange("p (j k) -> p j k", j=2)
        onehot = cut(P, T * P).rearrange("p (t q) -> p t q", t=T)
        oh_row = cut(P, P)
        oh_blk = cut(P, T)
        oh_s = cut(P, T)
        msg = cut(P, D)
        rows = cut(P, NW)
        a_dst = cut(P, 1)
        score = cut(P, 1)
        general_scores = cut(P, T)
        gidx = cut(P, 1).bitcast(I32)
        aidx = cut(P, 1).bitcast(I32)
        iota_f = sb("iota_f", [128, D])
        small_i = sb("small_i", [128, D], I32)
        part_i = sb("part_i", [128, 1], I32)
        wa2 = nb[:, 0:L * D].rearrange("q (l d) -> q l d", l=L)
        prod = nb[:, L * D:(L + 1) * D]
        samp_i = nb[0:P, (L + 1) * D:(L + 1) * D + T * BLOCK].bitcast(I32).rearrange("p (b e) -> p b e", b=T)
        wins = ab[:, 0:COLS * P // 2 + 1].bitcast(F16)[:, 0:COLS * P]
        COUNT_SPLIT = [(i * COLS * P // 4, (i + 1) * COLS * P // 4) for i in range(4)]
        count_row = so[0:1, :, :].rearrange("p t d -> p (t d)")[:, 0:COLS * P]
        win_i = sb("win_i", [P, COLS], I32)
        first_t = sb("first_t", [P, COLS])
        samp = sb("samp", [P, T])
        bidx_f = sb("bidx_f", [P, COLS])
        bidx = sb("bidx", [P, COLS], I32)
        assert NBLK == P * T

        node_table = nc.dram_tensor("node_table", [N, NW], F32).ap()
        h_table = nc.dram_tensor("h_table", [N, D], F32).ap()
        a_table = nc.dram_tensor("a_table", [N, 1], F32).ap()
        x1_table = nc.dram_tensor("x1_table", [N, D], F32).ap()
        blocks = nc.dram_tensor("edge_blocks", [LASTB + 1, 3 * SLOTS], I32).ap()

        x_in_s = sem("x_loaded")
        w_in = sem("weights_loaded")
        samp_in = sem("samples_loaded")
        blocks_out = sem("edge_blocks_written")
        wins_ok = sem("window_numbers_ready")
        reps = sem("repeated_iota_ready")
        iotas = sem("iotas_ready")
        consts = sem("constants_ready")
        wide_ok = sem("wide_weights_ready")
        dchain = sem("vector_chain")
        caught_ok = sem("caught_counted")
        h_sb = sem("h_copied")
        C_h = sem("h_rows_copied")
        C_back = sem("sums_transposed")
        cmp_ok = sem("comparisons_ready")
        row_ps = sem("row_of_counts_ready")
        row_sb = sem("row_of_counts_copied")
        cnt_ok = sem("block_counts_ready")
        bidx_ok = sem("block_indices_ready")
        fetch_in = sem("edges_fetched")
        prep_ok = [sem(f"edge_array_ready{a}") for a in range(5)]
        as_float = sem("edges_as_floats")
        hi_ok = sem("sources_n_over_T_ready")
        delta_ok = sem("target_distances_ready")
        square_ok = sem("squares_ready")
        rest_ok = sem("weight_remainders_ready")
        et_ps = sem("edge_transposes_ready")
        et_sb = sem("edge_transposes_copied")
        sum_ps = sem("caught_summed")
        flag_ok = sem("flag_ready")
        xt_ps = sem("x_transposed")
        xt_sv = sem("x_transposes_copied_by_vector")
        xt_sa = sem("x_transposes_copied_by_scalar")
        nb_ps = sem("node_products_ready")
        nb_sb = sem("node_products_copied")
        a_ps = sem("a_products_ready")
        a_sb = sem("a_copied")
        new_x = sem("features_ready")
        A_hot = sem("C_onehots_ready")
        A_bank = sem("C_banks_ready")
        A_ev = sem("C_banks_copied")
        B_s = [sem(f"scores_ready{l}") for l in range(L)]
        B_p = [sem(f"counted_scores_ready{l}") for l in range(L)]
        B_mm = [sem(f"attention_steps_done{l}") for l in range(L)]
        B_ev = [sem(f"sums_copied{l}") for l in range(L)]
        C_hot = sem("W_onehots_ready")
        C_key = sem("W_keys_ready")
        C_bank = sem("W_banks_ready")
        C_ev = sem("W_banks_copied")
        C_t = sem("W_transposes_ready")
        C_tev = sem("W_transposes_copied")
        C_o = sem("out_products_ready")
        C_add = sem("out_products_added")
        tab = sem("tables_written")
        x0_in = sem("input_reloaded")
        x1_out = sem("x1_written")
        x1_in = sem("x1_loaded")
        g_in = sem("general_edges_loaded")
        g_idx = [sem(f"g_indices{l}") for l in range(PASSES)]
        g_go = [sem(f"g_go{l}") for l in range(PASSES)]
        g_rows = [sem(f"g_rows{l}") for l in range(PASSES)]
        g_score = [sem(f"g_score{l}") for l in range(PASSES)]
        g_hot = [sem(f"g_hot{l}") for l in range(PASSES)]
        g_oh = [sem(f"g_onehot{l}") for l in range(PASSES)]
        g_msg = [sem(f"g_messages{l}") for l in range(PASSES)]
        g_used = [sem(f"g_chunks_done{l}") for l in range(PASSES)]
        g_chain = sem("g_vector_chain")
        pre_gelu = sem("pre_gelu_ready")
        gelu_ok = sem("gelu_ready")
        half_ok = sem("minus_half_ready")
        pchain = sem("pool_chain")
        mean_ok = sem("means_ready")
        res_ok = sem("residuals_ready")
        stats_ok = sem("statistics_ready")
        rstd_ok = sem("rstd_ready")
        fin_ok = sem("output_rows_ready")
        out_ok = sem("out_written")

        block = ctx.enter_context(nc.Block())
        tiles = "(t p) d -> p t d"
        hl = "(p t) d -> p t d"
        LOADS = 16 * (9 * L + 2)
        NJ = T // JT
        USES = [range(l * NJ, (l + 1) * NJ + (NJ if l == L - 1 else 0)) for l in range(L)]
        USES.append(range(USES[-1].stop, USES[-1].stop + BANKFULS))
        g_steps = [0]
        p_steps = [0]

        def is_fast(eng):
            eng.wait_ge(flag_ok, 1)
            return eng.value_load(fast_i[0:1, 0:1], min_val=0, max_val=1)

        RUN = 8

        MIX = {"vector": [0, 1, None, None], "tensor": [0, 1, 2, None, None], "scalar": [None, None, 0, 1, 2]}

        LEAD = 1
        assert GROUPS + LEAD <= 5 * COLS

        def steps_loop(eng, step, hook, mix=None, group=None, lead=0, peeled=()):
            for j in range(T // JT):
                G = READY[j] + lead
                hook(j, 0)
                extra = group is not None and j + 1 < T // JT and READY[j + 1] - READY[j] > RUN // 2 * 3
                if extra and mix[0] is not None:
                    whole(group, mix, G, G % 2)
                step(j * T, j, 0, (j * T) % 2, True)
                if extra and mix[0] is None:
                    whole(group, mix, G, G % 2)
                G += extra
                for h in range(3):
                    hook(j, h + 1)
                    n, r = j * T + 1 + h * RUN, 1 + h * RUN

                    def pair(i):
                        for u in range(2):
                            step(i * 2 + (n + u), j, i * 2 + (r + u), (n + u) % 2, False)

                    def mixed(i):
                        for u in range(2):
                            m = 2 * u
                            for part in mix:
                                if part is None:
                                    step(i * 4 + (n + m), j, i * 4 + (r + m), (n + m) % 2, False)
                                    m += 1
                                else:
                                    group(i * 2 + (G + u), (G + u) % 2, part)

                    body, count = (pair, RUN // 2) if group is None or j + 1 == T // JT else (mixed, RUN // 4)
                    start = 1 if h in peeled else 0
                    if start:
                        body(0)
                    with eng.Fori(start, count) as i:
                        body(i)
                    if body is mixed:
                        G += RUN // 2
                hook(j, 4)

        def whole(group, mix, G, slot):
            for part in mix:
                if part is not None:
                    group(G, slot, part)

        def first_groups(eng, group, mix, lead=0):
            first = READY[0] + lead
            with eng.Fori(0, first // 2) as i:
                whole(group, mix, i * 2, 0)
                whole(group, mix, i * 2 + 1, 1)
            for G in range(first // 2 * 2, first):
                whole(group, mix, G, G % 2)

        LAST = COLS - 1
        LAST_G = GROUPS - 5 * LAST

        def columns_loop(eng, body):
            body(0, 0, 5, 0)
            body(1, 1, 5, 1)
            with eng.Fori(0, (LAST - 2) // 2) as i:
                body(i * 2 + 2, 0, 5, 2)
                body(i * 2 + 3, 1, 5, 2)
            for s in range(2 + 2 * ((LAST - 2) // 2), LAST):
                body(s, s % 2, 5, 2)
            body(LAST, LAST % 2, LAST_G, 2)

        def behind_items(ks):
            items = []
            for q in range(BANKFULS):
                items += [("turn", q, k) for k in range(ks)]
                if q:
                    items.append(("product", q - 1, ks))
            return items + [("product", BANKFULS - 1, ks)]

        def column_items(ng, behind):
            builds = [("build", g, i) for g in range(ng) for i in range(3)]
            if not behind:
                return builds
            work, items, n = behind_items(2), [], 0
            for m, b in enumerate(builds):
                items.append(b)
                upto = n if m % 3 != 1 else (m + 2) * len(work) // len(builds)
                items += work[n:upto]
                n = upto
            return items

        def products_in(ng, g):
            at, found = -1, []
            for kind, a, b in column_items(ng, 1):
                if kind == "build":
                    at = a
                elif kind == "product" and at == g:
                    found.append(a)
            return found

        def span(q):
            return range(q * PER_BANK, min(T, (q + 1) * PER_BANK))

        FREE_A, FREE_AEV = 4, 3
        FREE_B = 2
        FREE_C, FREE_CEV, FREE_T, FREE_TEV, FREE_O, FREE_ADD = 4, 3, 14, 2, 7, 7

        NBU = -(-T // 3)
        U_ALL = NBU + 2 * BANKFULS

        def general_loads(sp, l):
            if l == 0:
                sp.wait_ge(A_ev, 3 * READY[0] + FREE_AEV)
                sp.dma_start(src_i, src.rearrange("(p k) -> p k", k=K)).then_inc(g_in, 16)
                sp.dma_start(dst_i, dst.rearrange("(p k) -> p k", k=K)).then_inc(g_in, 16)
                sp.dma_start(wgt, edge_weight.rearrange("(p k) -> p k", k=K)).then_inc(g_in, 16)
            if l < L:
                sp.wait_ge(nb_sb, (NBU + BANKFULS) * (l + 1))
                sp.dma_start(node_table.rearrange(hl, t=T), NB).then_inc(tab, 16)
                sp.wait_ge(a_sb, BANKFULS * (l + 1))
                sp.dma_start(a_table.rearrange("(o n) d -> o (n d)", o=1), ab[0:1, 0:N]).then_inc(tab, 16)
            else:
                sp.wait_ge(h_sb, BANKFULS)
                sp.dma_start(h_table.rearrange(tiles, p=P), so[:]).then_inc(tab, 16)
            sp.wait_ge(tab, 32 * (l + 1) if l < L else 32 * L + 16)

        @block.sync
        def _(sp):
            sp.dma_start(samp_i, dst.rearrange("(p b e) -> p b e", b=T, e=BLOCK)).then_inc(samp_in, 16)
            for f, a in enumerate((src, dst, edge_weight.bitcast(I32))):
                over = bass.AP(a.tensor, 0, [[BLOCK, LASTB + 1], [1, SLOTS]])
                sp.dma_start(blocks[:, f * SLOTS:(f + 1) * SLOTS], over).then_inc(blocks_out, 16)

            fast = is_fast(sp)
            for l in range(PASSES):
                with sp.If(fast == 0):
                    general_loads(sp, l)
                if l == L - 1:
                    sp.wait_ge(pre_gelu, l * T // JT)
                    sp.dma_start(x_in, x.rearrange(tiles, p=P)).then_inc(x0_in, 16)
                    sp.wait_ge(new_x, L * T // JT)
                    sp.dma_start(x1_table.rearrange(tiles, p=P), xs[:]).then_inc(x1_out, 16)
                    sp.wait_ge(x1_out, 16)
                    sp.dma_start(tmp, x1_table.rearrange(hl, t=T)).then_inc(x1_in, 16)
            for q in range(BANKFULS):
                t = span(q)
                sp.wait_ge(fin_ok, q + 1)
                sp.dma_start(out.rearrange(hl, t=T)[:, t.start:t.stop, :], so[:, t.start:t.stop, :]).then_inc(out_ok, 16)
            sp.wait_ge(out_ok, 16 * BANKFULS)
            sp.wait_ge(blocks_out, 48)

        def use_of(l, j, second):
            return USES[l][2 * j + second] if l == L - 1 else USES[l][j]

        def of_group(a, j):
            return a[:, j * JT:(j + 1) * JT, :]

        def along_group(a, l):
            return a[:, l, :].unsqueeze(1).to_broadcast([P, JT, D])

        def inverse_deviation(pool, m):
            pool.wait_ge(stats_ok, m + 1)
            nc.gpsimd.tensor_tensor(rstd[:, m % 2, :], veps[:, m % 2, :], minus_half[:], ALU.pow).then_inc(rstd_ok, 1)
            pool.wait_ge(rstd_ok, m + 1)

        def pool_finish(pool, l):
            def link(ins):
                ins.then_inc(pchain, 1)
                p_steps[0] += 1
                pool.wait_ge(pchain, p_steps[0])

            def normalised(j, m):
                y, b = of_group(xs, j), m % 2
                inverse_deviation(pool, m)
                link(nc.gpsimd.tensor_tensor(y, y, mv[:, b, :, 0].unsqueeze(2).to_broadcast([P, JT, D]), ALU.subtract))
                return nc.gpsimd.tensor_tensor(y, y, rstd[:, b, :].unsqueeze(2).to_broadcast([P, JT, D]), ALU.mult)

            def outer(j):
                normalised(j, use_of(l, j, 1)).then_inc(new_x, 1)

            for j in range(NJ - 1):
                y, u = of_group(xs, j), of_group(accum, j)
                pool.wait_ge(mean_ok, l * (NJ - 1) + j + 1)
                nc.gpsimd.tensor_tensor(u, u, of_group(so, j), ALU.add).then_inc(pre_gelu, 1)
                if l == L - 1 and j:
                    outer(j - 1)
                pool.wait_ge(gelu_ok, l * NJ + j + 1)
                nc.gpsimd.tensor_tensor(y, y, u, ALU.add).then_inc(res_ok, 1)
                link(normalised(j, use_of(l, j, 0)))
                link(nc.gpsimd.tensor_tensor(y, y, along_group(gam, l), ALU.mult))
                last = nc.gpsimd.tensor_tensor(y, y, along_group(bet, l), ALU.add)
                if l < L - 1:
                    last.then_inc(new_x, 1)
                else:
                    link(last)
                    pool.wait_ge(x0_in, 16)
                    nc.gpsimd.tensor_tensor(y, y, of_group(x_in, j), ALU.add).then_inc(res_ok, 1)
            if l == L - 1:
                outer(NJ - 2)
            inverse_deviation(pool, use_of(l, NJ - 1, 0))
            if l == L - 1:
                inverse_deviation(pool, use_of(l, NJ - 1, 1))

        @block.gpsimd
        def _(pool):
            nc.gpsimd.iota(wins, pattern=[[1, COLS * P]], base=0, channel_multiplier=0, allow_small_or_imprecise_dtypes=True).then_inc(wins_ok, 1)
            nc.gpsimd.iota(small_i[:], pattern=[[1, D]], base=0, channel_multiplier=0).then_inc(iotas, 1)
            nc.gpsimd.iota(part_i[:], pattern=[[0, 1]], base=0, channel_multiplier=1).then_inc(iotas, 1)
            nc.gpsimd.iota(win_i[:], pattern=[[WIN * P, COLS]], base=0, channel_multiplier=WIN).then_inc(iotas, 1)
            nc.gpsimd.memset(edgesT[:].rearrange("q a w -> q (a w)").bitcast(I32), 0).then_inc(reps, 1)
            nc.gpsimd.iota(iota_rep[:], pattern=[[1, HV], [0, GP]], base=0, channel_multiplier=0, allow_small_or_imprecise_dtypes=True).then_inc(reps, 1)
            nc.gpsimd.memset(minus_half[:], -0.5).then_inc(half_ok, 1)
            pool.wait_ge(blocks_out, 48)
            pool.wait_ge(bidx_ok, 1)
            for c in range(COLS):
                pool.indirect_dma_start(fetched[:, c].rearrange("p f e -> p (f e)"), None, blocks,
                                        bass.IndirectOffsetOnAxis(bidx[:, c:c + 1], 0)).then_inc(fetch_in, 16)
            pool.wait_ge(half_ok, 1)
            pool.wait_ge(fetch_in, 16 * COLS)
            pool.wait_ge(prep_ok[2], 1)
            nc.gpsimd.tensor_tensor(e_f[4], fetched[:, :, 2, :].bitcast(F32), e_16[2], ALU.subtract).then_inc(rest_ok, 1)
            pool.wait_ge(prep_ok[3], 1)
            nc.gpsimd.tensor_tensor(e_f[5], e_f[4], e_16[3], ALU.subtract).then_inc(rest_ok, 1)
            fast = is_fast(pool)
            for l in range(PASSES):
                with pool.If(fast == 0):
                    pool.wait_ge(tab, 32 * (l + 1) if l < L else 32 * L + 16)
                    with pool.Fori(0, K) as k:
                        pool.wait_ge(g_idx[l], k * 2 + 2)
                        pool.wait_ge(g_msg[l], k + 1)
                        pool.sem_inc(g_go[l], 1)
                        if l < L:
                            pool.indirect_dma_start(rows, None, node_table, bass.IndirectOffsetOnAxis(gidx, 0)).then_inc(g_rows[l], 16)
                            pool.indirect_dma_start(a_dst, None, a_table, bass.IndirectOffsetOnAxis(aidx, 0)).then_inc(g_rows[l], 16)
                        else:
                            pool.indirect_dma_start(rows[:, 0:D], None, h_table, bass.IndirectOffsetOnAxis(gidx, 0)).then_inc(g_rows[l], 16)
                    for m in USES[l]:
                        inverse_deviation(pool, m)
                with pool.If(fast == 1):
                    if l < L:
                        pool_finish(pool, l)
                    else:
                        for m in USES[l]:
                            inverse_deviation(pool, m)

        def nb_row(r, c0, c1):
            if isinstance(r, int):
                return NB[:, r, c0:c1]
            return nb[0:P, 0:T * NW].rearrange("p (t d) -> p t d", d=NW)[:, bass.ds(r, 1), c0:c1].rearrange("p o d -> p (o d)")

        def count_group_on(pe):
            def group(G, slot, i):
                w0, w1 = SPLIT[i]
                pe.wait_ge(A_hot, G + 1)
                pe.wait_ge(A_ev, G * 3 + (i + 1))
                for w in range(w0, w1):
                    last = pe.matmul(ps[:, 4 + i, (w - w0) * KEYS:(w - w0 + 1) * KEYS], HI[:, slot, :, w],
                                     KEY[:, slot, :, w], start=True, stop=True)
                last.then_inc(A_bank, 1)

            return group

        def attention_products(pe, l, group):
            pe.sem_inc(B_mm[l], FREE_B)

            def hook(j, h):
                if h == 0 and j >= 2:
                    pe.wait_ge(B_ev[l], j - 1)

            def step(n, j, r, slot, first):
                pe.wait_ge(B_p[l], n + 1 + FREE_B)
                for k in range(JT):
                    last = pe.matmul(ps[0:P, 2 * (j % 2) + k // 3, (k % 3) * (D + 1):(k % 3 + 1) * (D + 1)],
                                     PR[slot][:, k * P:(k + 1) * P], nb_row(r, 0, D + 1),
                                     start=(first and k % 3 == 0), stop=False, skip_group_check=True)
                last.then_inc(B_mm[l], 1)

            steps_loop(pe, step, hook, MIX["tensor"], group, LEAD)

        def last_products(pe):
            pe.sem_inc(C_bank, FREE_C)
            pe.sem_inc(C_t, FREE_T)
            pe.sem_inc(C_o, FREE_O)

            def build(G, slot, i):
                w0, w1 = SPLIT[i]
                pe.wait_ge(C_hot, G + 1)
                pe.wait_ge(C_ev, G * 3 + (i + 1))
                for w in range(w0, w1):
                    for j in range(3):
                        last = pe.matmul(ps[:, i, (w - w0) * KEYS:(w - w0 + 1) * KEYS], HI[:, slot, :, w],
                                         KW[:, slot, :, j, w], start=(j == 0), stop=(j == 2))
                last.then_inc(C_bank, 1)

            def turn(par, q, k, evacs, n, bank):
                pe.wait_ge(C_ev, evacs)
                pe.wait_ge(C_tev, n + 1)
                for r in span(q):
                    last = pe.transpose(ps[0:P, bank, (r % PER_BANK) * P:(r % PER_BANK + 1) * P],
                                        W[par][:, r, k * P:(k + 1) * P], ident[0:P, 0:P])
                last.then_inc(C_t, 1)

            def product(sp, par, q, ks, turned):
                pe.wait_ge(C_tev, turned)
                if q == 0:
                    pe.wait_ge(C_h, sp + 1)
                pe.wait_ge(C_add, sp * 7 + (FREE_ADD + (q - 2 if q >= 3 else (0, -2, -1)[q])))
                n = len(span(q)) * P
                for k in range(ks):
                    last = pe.matmul(ps[:, 5 + q % 3, 0:n], hcur[:, par, k, :],
                                     WT[k][:, q * PER_BANK:q * PER_BANK + len(span(q)), :].rearrange("p r c -> p (r c)"),
                                     start=(k == 0), stop=(k == ks - 1))
                last.then_inc(C_o, 1)

            def column(s, par, ng, behind):
                for kind, a, b in column_items(ng, behind):
                    if kind == "build":
                        build(s * 5 + a, (par + a) % 2, b)
                    elif kind == "turn":
                        turn(1 - par, a, b, s * 15 + FREE_CEV, (s - 1) * 14 + (2 * a + b), 3 + b)
                    else:
                        product(s - 1, 1 - par, a, 2, (s - 1) * 14 + (2 * a + 2 + FREE_TEV))

            columns_loop(pe, column)
            for kind, a, b in behind_items(1):
                if kind == "turn":
                    turn(LAST % 2, a, b, LAST * 15 + 3 * LAST_G + FREE_CEV, LAST * 14 + a, 3 + a % 2)
                else:
                    product(LAST, LAST % 2, a, 1, LAST * 14 + a + 1 + FREE_TEV)
            pe.wait_ge(C_add, 7 * (LAST + 1) + FREE_ADD)
            for q in range(BANKFULS):
                for r in span(q):
                    last = pe.transpose(ps[0:P, q, (r % PER_BANK) * D:(r % PER_BANK + 1) * D], accT[:, r * P:(r + 1) * P], ident[:])
                last.then_inc(C_back, 1)

        def general_products(pe, l):
            def chunk(k, first):
                pe.wait_ge(g_oh[l], k + 1)
                pe.wait_ge(g_msg[l], k + 2)
                for t in range(T):
                    last = pe.matmul(ps[0:P, t // PER_BANK, (t % PER_BANK) * D:(t % PER_BANK + 1) * D], onehot[:, t, :], msg,
                                     start=(first and t % PER_BANK == 0), stop=False, skip_group_check=True)
                if l < L:
                    last = pe.matmul(ps[0:P, 7, 0:T], oh_row, oh_s, start=first, stop=False, skip_group_check=True)
                last.then_inc(g_used[l], 1)

            pe.sem_inc(g_used[l], 1)
            chunk(0, True)
            with pe.Fori(1, K) as k:
                chunk(k, False)

        @block.tensor
        def _(pe):
            count_group = count_group_on(pe)
            pe.wait_ge(consts, 1)
            for b in range(T):
                pe.wait_ge(cmp_ok, b + 1)
                for i, (w0, w1) in enumerate(COUNT_SPLIT):
                    last = pe.matmul(ps[0:1, 4 + i, 0:w1 - w0], ones16[:], cmp_[:, b, w0:w1], start=(b == 0), stop=(b == T - 1))
            last.then_inc(row_ps, 1)

            def nodes(l):
                pe.wait_ge(x_in_s, 16)
                pe.wait_ge(consts, 2)
                if l:
                    pe.wait_ge(B_ev[l - 1], NJ)
                for q in range(BANKFULS):
                    if l == 0 and q == 4:
                        pe.wait_ge(row_sb, 2)
                        for c in range(COLS):
                            last = pe.matmul(ps[0:P, 7, c:c + 1], count_row[:, c * P:(c + 1) * P], ones[0:1, 0:1],
                                             start=True, stop=True)
                        last.then_inc(cnt_ok, 1)
                    if l:
                        pe.wait_ge(new_x, (l - 1) * NJ + span(q)[-1] // JT + 1)
                    for t in span(q):
                        last = pe.transpose(ps[:, q, (t % PER_BANK) * P:(t % PER_BANK + 1) * P], xs[:, t, :], ident[0:P, 0:P])
                    last.then_inc(xt_ps, 1)
                pe.wait_ge(xt_sv, 4 * (l + 1))
                pe.wait_ge(xt_sa, 3 * (l + 1))
                pe.wait_ge(w_in, LOADS)
                if l == L:
                    for q in range(BANKFULS):
                        for t in span(q):
                            last = pe.matmul(ps[0:P, q, (t % PER_BANK) * D:(t % PER_BANK + 1) * D],
                                             xT[:, t * P:(t + 1) * P], kern[:], start=True, stop=True)
                        last.then_inc(nb_ps, 1)
                    return
                pe.wait_ge(wide_ok, L)
                for u in range(U_ALL):
                    if u >= 7:
                        pe.wait_ge(nb_sb, (NBU + BANKFULS) * l + u - 6)
                    if u < NBU:
                        for r in range(3 * u, min(T, 3 * u + 3)):
                            last = pe.matmul(ps[0:P, u % 7, (r % 3) * NW:(r % 3 + 1) * NW], xT[:, r::T], wideN[:, l, :], start=True, stop=True)
                        last.then_inc(nb_ps, 1)
                    elif u < NBU + BANKFULS:
                        for t in span(u - NBU):
                            last = pe.matmul(ps[0:P, u % 7, (t % PER_BANK) * D:(t % PER_BANK + 1) * D], xT[:, t * P:(t + 1) * P],
                                             wideS[:, l, :], start=True, stop=True)
                        last.then_inc(nb_ps, 1)
                    else:
                        q = u - NBU - BANKFULS
                        n = len(span(q)) * P
                        pe.matmul(ps[0:P, u % 7, 0:n], wa1_rep[:, l, :], xT[:, q * PER_BANK * P:q * PER_BANK * P + n],
                                  start=True, stop=True).then_inc(a_ps, 1)

            nodes(0)

            pe.wait_ge(nb_sb, NBU + BANKFULS)
            pe.wait_ge(a_sb, BANKFULS)
            for u in range(10):
                a, half = u // 2, u % 2
                pe.wait_ge(prep_ok[a], 1)
                if u >= 7:
                    pe.wait_ge(et_sb, u - 6)
                cs = range(8) if half == 0 else range(8, COLS)
                for j, c in enumerate(cs):
                    last = pe.transpose(ps[:, u % 7, :].bitcast(BF16)[:, j * 128:j * 128 + P], e_16[a][:, c, :], ident16[0:P, 0:P])
                last.then_inc(et_ps, 1)
            pe.wait_ge(caught_ok, 1)
            pe.wait_ge(bidx_ok, 1)
            pe.matmul(ps[0:1, 7, 0:1], caught[:], ones[:], start=True, stop=True).then_inc(sum_ps, 1)

            pe.wait_ge(et_sb, 10)
            pe.sem_inc(A_bank, FREE_A)

            first_groups(pe, count_group, MIX["tensor"], LEAD)

            fast = is_fast(pe)
            for l in range(PASSES):
                if l:
                    nodes(l)
                if l < L:
                    pe.wait_ge(nb_sb, (NBU + BANKFULS) * (l + 1))
                    pe.wait_ge(a_sb, BANKFULS * (l + 1))
                else:
                    pe.wait_ge(h_sb, BANKFULS)
                with pe.If(fast == 1):
                    if l < L:
                        attention_products(pe, l, count_group if l == 0 else None)
                    else:
                        last_products(pe)
                with pe.If(fast == 0):
                    general_products(pe, l)

        def gelu(act, l, j):
            act.wait_ge(pre_gelu, l * NJ + j + 1)
            u = accum[:, j * JT:(j + 1) * JT, :]
            nc.scalar.activation(u, u, ACT.Gelu).then_inc(gelu_ok, 1)

        def count_copies_on(act):
            def group(G, slot, i):
                w0, w1 = SPLIT[i]
                act.wait_ge(A_bank, G * 3 + (i + 1 + FREE_A))
                n = (w1 - w0) * WIN
                nc.scalar.copy(C[:, :, bass.ds(G * GC + WIN * w0, n)] if not isinstance(G, int) else
                               C[:, :, G * GC + WIN * w0:G * GC + WIN * w0 + n],
                               ps[0:P, 4 + i, 0:n * T].rearrange("p (c r) -> p r c", r=T)).then_inc(A_ev, 1)

            return group

        def attention_scores(act, l, group):
            def hook(j, h):
                if h == 2 and j:
                    gelu(act, l, j - 1)

            def step(n, j, r, slot, first):
                act.wait_ge(B_p[l], n + 1)
                nc.scalar.activation(S[slot], ab[:, j * JC:(j + 1) * JC], ACT.Sigmoid, bias=nb_row(r, B, B + 1)).then_inc(B_s[l], 1)

            act.wait_ge(nb_sb, (NBU + BANKFULS) * (l + 1))
            act.wait_ge(a_sb, BANKFULS * (l + 1))
            steps_loop(act, step, hook, MIX["scalar"], group, peeled=(1,))
            gelu(act, l, NJ - 1)

        def last_copies(act):
            act.sem_inc(C_ev, FREE_CEV)
            act.sem_inc(C_tev, FREE_TEV)
            act.wait_ge(new_x, L * NJ)
            act.wait_ge(h_sb, BANKFULS)

            def build(G, g, par, i):
                w0, w1 = SPLIT[i]
                act.wait_ge(C_bank, G * 3 + (i + 1 + FREE_C))
                n = (w1 - w0) * WIN
                c0 = g * GC + WIN * w0
                nc.scalar.copy(W[par][:, :, c0:c0 + n], ps[0:P, i, 0:n * T].rearrange("p (c r) -> p r c", r=T)).then_inc(C_ev, 1)

            def turn(sp, q, k, n, bank):
                act.wait_ge(C_t, n + (1 + FREE_T))
                act.wait_ge(C_o, sp * 7 + (q + 1))
                m = len(span(q))
                nc.scalar.copy(WT[k][:, q * PER_BANK:q * PER_BANK + m, :],
                               ps[0:P, bank, 0:m * P].rearrange("p (r c) -> p r c", c=P)).then_inc(C_tev, 1)

            def rows_of_h(s, par, ks, behind):
                if behind:
                    act.wait_ge(C_o, s * 7)
                h = so[:, bass.ds(s * 2, ks), :] if not isinstance(s, int) else so[:, 2 * s:2 * s + ks, :]
                nc.scalar.copy(hcur[:, par, 0:ks, :], h).then_inc(C_h, 1)

            def column(s, par, ng, behind):
                rows_of_h(s, par, 2 if ng == 5 else 1, behind)
                if behind:
                    act.wait_ge(C_t, s * 14)
                for kind, a, b in column_items(ng, behind):
                    if kind == "build":
                        build(s * 5 + a, a, par, b)
                    elif kind == "turn":
                        turn(s - 1, a, b, (s - 1) * 14 + (2 * a + b), 3 + b)

            columns_loop(act, column)
            for q in range(BANKFULS):
                turn(LAST, q, 0, LAST * 14 + q, 3 + q % 2)

        @block.scalar
        def _(act):
            act.dma_start(xs[:], x.rearrange(tiles, p=P)).then_inc(x_in_s, 16)
            for l in range(L):
                act.dma_start(wideN[:, l, 0:D], Wn[l]).then_inc(w_in, 16)
                act.dma_start(wideS[:, l, :], Ws[l]).then_inc(w_in, 16)
                act.dma_start(wa1[:, l:l + 1], Wa[l, 0:D].unsqueeze(1)).then_inc(w_in, 16)
                act.dma_start(wa2[:, l, :], Wa[l, D:2 * D].partition_broadcast(D)).then_inc(w_in, 16)
                act.dma_start(biasN[:, l, 0:D], bn[l].partition_broadcast(P)).then_inc(w_in, 16)
                act.dma_start(biasS[:, l, :], bs[l].partition_broadcast(P)).then_inc(w_in, 16)
                act.dma_start(ba_b[:, l:l + 1], ba[l:l + 1].partition_broadcast(P)).then_inc(w_in, 16)
                act.dma_start(gam[:, l, :], gamma[l].partition_broadcast(P)).then_inc(w_in, 16)
                act.dma_start(bet[:, l, :], beta[l].partition_broadcast(P)).then_inc(w_in, 16)
            act.dma_start(kern[:], kernel1).then_inc(w_in, 16)
            act.dma_start(bi1[:], bias1.partition_broadcast(P)).then_inc(w_in, 16)

            def nodes(l):
                for q in range(1, BANKFULS, 2):
                    n = len(span(q)) * P
                    act.wait_ge(xt_ps, l * BANKFULS + q + 1)
                    nc.scalar.copy(xT[:, q * PER_BANK * P:q * PER_BANK * P + n], ps[:, q, 0:n]).then_inc(xt_sa, 1)
                if l == L:
                    for q in range(BANKFULS):
                        t = span(q)
                        act.wait_ge(nb_ps, (NBU + BANKFULS) * L + q + 1)
                        nc.scalar.copy(so[:, t.start:t.stop, :], ps[0:P, q, 0:len(t) * D].rearrange("p (t d) -> p t d", d=D)).then_inc(h_sb, 1)
                    return
                act.wait_ge(w_in, LOADS)
                act.wait_ge(cmp_ok, T)
                for q in range(BANKFULS):
                    n = len(span(q)) * P
                    act.wait_ge(a_ps, l * BANKFULS + q + 1)
                    nc.scalar.activation(ab[:, q * PER_BANK * P:q * PER_BANK * P + n], ps[0:P, (q + NBU + BANKFULS) % 7, 0:n], ACT.Identity,
                                         bias=ba_b[:, l:l + 1]).then_inc(a_sb, 1)

            act.wait_ge(row_ps, 1)
            for i in (2, 3):
                w0, w1 = COUNT_SPLIT[i]
                last = nc.scalar.copy(count_row[:, w0:w1], ps[0:1, 4 + i, 0:w1 - w0])
            last.then_inc(row_sb, 1)
            nodes(0)
            act.wait_ge(fetch_in, 16 * COLS)
            nc.scalar.copy(e_f[0], fetched[:, :, 0, :]).then_inc(as_float, 1)
            nc.scalar.copy(e_f[2], fetched[:, :, 1, :]).then_inc(as_float, 1)
            nc.scalar.copy(e_16[2], fetched[:, :, 2, :].bitcast(F32)).then_inc(prep_ok[2], 1)
            act.wait_ge(hi_ok, 1)
            nc.scalar.copy(e_16[0], e_f[1]).then_inc(prep_ok[0], 1)
            act.wait_ge(rest_ok, 1)
            nc.scalar.copy(e_16[3], e_f[4]).then_inc(prep_ok[3], 1)
            act.wait_ge(delta_ok, 1)
            act.wait_ge(half_ok, 1)
            nc.scalar.activation(e_f[3], e_f[2], ACT.Square, bias=minus_half[:, 0:1]).then_inc(square_ok, 1)
            act.wait_ge(reps, 1)
            for u in range(10):
                if u == 4:
                    act.wait_ge(rest_ok, 2)
                    nc.scalar.copy(e_16[4], e_f[5]).then_inc(prep_ok[4], 1)
                a, half = u // 2, u % 2
                c0, c1 = (0, 8) if half == 0 else (8, COLS)
                act.wait_ge(et_ps, u + 1)
                nc.scalar.copy(edgesT[:, a, c0 * 5 * GP:c1 * 5 * GP].rearrange("q (c g w) -> q c g w", g=5, w=GP)[:, :, :, 0:GW],
                               ps[:, u % 7, :].bitcast(BF16)[:, 0:(c1 - c0) * 128].rearrange("q (c w) -> q c w", w=128)[:, :, 0:P]
                               .rearrange("q c (g w) -> q c g w", w=GW)).then_inc(et_sb, 1)
            act.sem_inc(A_ev, FREE_AEV)
            act.wait_ge(prep_ok[1], 1)
            act.wait_ge(caught_ok, 1)

            count_copies = count_copies_on(act)
            first_groups(act, count_copies, MIX["scalar"])

            fast = is_fast(act)
            for l in range(PASSES):
                if l:
                    nodes(l)
                with act.If(fast == 1):
                    if l < L:
                        attention_scores(act, l, count_copies if l == 0 else None)
                    else:
                        last_copies(act)
                if l < L:
                    with act.If(fast == 0):
                        with act.Fori(0, K) as k:
                            act.wait_ge(g_rows[l], k * 32 + 32)
                            nc.scalar.activation(score, rows[:, B:B + 1], ACT.Sigmoid, bias=a_dst).then_inc(g_score[l], 1)
                        for j in range(NJ):
                            gelu(act, l, j)

        def statistics(dve, link, y, m, n):
            for t in range(n):
                last = nc.vector.bn_stats(stats[:, t, :], y[:, t, :])
            link(last)
            for t in range(n):
                last = nc.vector.bn_aggr(mv[:, m % 2, t, :], stats[:, t, :])
            link(last)
            nc.vector.tensor_scalar(veps[:, m % 2, :], mv[:, m % 2, :, 1], EPS_NORM, None, ALU.add).then_inc(stats_ok, 1)

        def normalise(dve, y, m, n):
            dve.wait_ge(rstd_ok, m + 1)
            for t in range(n):
                last = nc.vector.tensor_scalar(y[:, t, :], y[:, t, :], mv[:, m % 2, t, 0:1], rstd[:, m % 2, t:t + 1],
                                               ALU.subtract, ALU.mult)
            return last

        def finish_mean(dve, link, l, j, parts, banks_free, by_pool=False):
            u = accum[:, j * JT:(j + 1) * JT, :]
            for sums, scores, t, n in parts:
                last = nc.vector.tensor_scalar(den[:, t:t + n], scores, EPS_SCORE, None, ALU.add)
            link(last)
            d = den[:, parts[0][2]:parts[0][2] + JT]
            link(nc.vector.reciprocal(d, d))
            for sums, scores, t, n in parts:
                last = nc.vector.tensor_tensor(accum[:, t:t + n, :], sums, den[:, t:t + n].unsqueeze(2).to_broadcast([P, n, D]), ALU.mult)
            link(last)
            dve.sem_inc(banks_free, 1)
            if by_pool:
                dve.sem_inc(mean_ok, 1)
            else:
                nc.vector.tensor_tensor(u, u, of_group(so, j), ALU.add).then_inc(pre_gelu, 1)

        def finish_residual(dve, link, l, j):
            x_j, u = xs[:, j * JT:(j + 1) * JT, :], accum[:, j * JT:(j + 1) * JT, :]
            dve.wait_ge(gelu_ok, l * NJ + j + 1)
            link(nc.vector.tensor_tensor(x_j, x_j, u, ALU.add))
            statistics(dve, link, x_j, use_of(l, j, 0), JT)

        def finish_norm(dve, link, l, j):
            x_j = xs[:, j * JT:(j + 1) * JT, :]
            link(normalise(dve, x_j, use_of(l, j, 0), JT))
            link(nc.vector.tensor_tensor(x_j, x_j, gam[:, l, :].unsqueeze(1).to_broadcast([P, JT, D]), ALU.mult))
            last = nc.vector.tensor_tensor(x_j, x_j, bet[:, l, :].unsqueeze(1).to_broadcast([P, JT, D]), ALU.add)
            if l < L - 1:
                last.then_inc(new_x, 1)
                return
            link(last)
            dve.wait_ge(x0_in, 16)
            link(nc.vector.tensor_tensor(x_j, x_j, x_in[:, j * JT:(j + 1) * JT, :], ALU.add))
            statistics(dve, link, x_j, use_of(l, j, 1), JT)

        def finish_outer(dve, l, j):
            if l == L - 1:
                normalise(dve, xs[:, j * JT:(j + 1) * JT, :], use_of(l, j, 1), JT).then_inc(new_x, 1)

        def gathered(a, G):
            if isinstance(G, int):
                return edgesT[:, a, G * GP:(G + 1) * GP].unsqueeze(1)
            return edgesT[:, a, bass.ds(G * GP, GP)].unsqueeze(1)

        def count_onehots_on(dve):
            def group(G, slot, part):
                if part == 0:
                    dve.wait_ge(A_bank, G * 3 + 1)
                    nc.vector.tensor_tensor(HI[:, slot], gathered(0, G).to_broadcast([128, HV, GP]), iota_rep[:], ALU.is_equal)
                    return
                nc.vector.tensor_tensor(KEY[:, slot], gathered(1, G).to_broadcast([128, KEYS, GP]), iota_rep[:, 0:KEYS, :],
                                        ALU.is_equal).then_inc(A_hot, 1)

            return group

        def attention_weights(dve, l, link, group):
            dve.sem_inc(B_p[l], FREE_B)

            def pool_statistics(j, second):
                n = 2 if l == L - 1 else 1
                dve.wait_ge(res_ok, l * (NJ - 1) + n * j + second + 1)
                if n == 1 and j >= 2:
                    dve.wait_ge(new_x, j - 1)
                if second and j >= 1:
                    dve.wait_ge(new_x, l * NJ + j)
                statistics(dve, link, of_group(xs, j), use_of(l, j, second), JT)

            def mean(j):
                dve.wait_ge(B_mm[l], (j + 1) * T + FREE_B)
                parts = []
                for b, t, n in ((2 * (j % 2), j * JT, 3), (2 * (j % 2) + 1, j * JT + 3, 2)):
                    v = ps[0:P, b, 0:n * (D + 1)].rearrange("p (t d) -> p t d", d=D + 1)
                    parts.append((v[:, :, 0:D], v[:, :, D], t, n))
                finish_mean(dve, link, l, j, parts, B_ev[l], by_pool=j < NJ - 1)

            def hook(j, h):
                if h == 0 and group is not None:
                    dve.wait_ge(A_ev, 3 * READY[j] + FREE_AEV)
                if h == 1 and j:
                    mean(j - 1)
                    if l == L - 1 and j > 1:
                        pool_statistics(j - 2, 1)
                if h == 3 and j:
                    pool_statistics(j - 1, 0)

            def step(n, j, r, slot, first):
                dve.wait_ge(B_s[l], n + 1)
                dve.wait_ge(B_mm[l], n + 1)
                c = C[:, r, j * JC:(j + 1) * JC] if isinstance(r, int) else C[:, bass.ds(r, 1), j * JC:(j + 1) * JC].rearrange("p o c -> p (o c)")
                nc.vector.tensor_tensor(PR[slot], S[slot], c, ALU.mult).then_inc(B_p[l], 1)

            steps_loop(dve, step, hook, MIX["vector"], group, LEAD)
            mean(NJ - 1)
            if l == L - 1:
                pool_statistics(NJ - 2, 1)
            if l < L - 1:
                dve.wait_ge(new_x, l * NJ + NJ - 2)
            finish_residual(dve, link, l, NJ - 1)
            if l == L - 1:
                dve.wait_ge(new_x, l * NJ + NJ - 1)
            finish_norm(dve, link, l, NJ - 1)
            finish_outer(dve, l, NJ - 1)

        def last_onehots(dve):
            dve.sem_inc(C_add, FREE_ADD)

            def build(G, slot):
                dve.wait_ge(C_bank, G * 3 + 1)
                nc.vector.tensor_tensor(KEY[:, slot], gathered(1, G).to_broadcast([128, KEYS, GP]), iota_rep[:, 0:KEYS, :],
                                        ALU.is_equal).then_inc(C_key, 1)
                nc.vector.tensor_tensor(HI[:, slot], gathered(0, G).to_broadcast([128, HV, GP]), iota_rep[:], ALU.is_equal)
                dve.wait_ge(C_key, G + 1)
                nc.vector.tensor_tensor(KW[:, slot], KEY[:, slot].unsqueeze(2).to_broadcast([128, KEYS, 3, GP]),
                                        (edgesT[:, 2:5, G * GP:(G + 1) * GP] if isinstance(G, int) else edgesT[:, 2:5, bass.ds(G * GP, GP)]).unsqueeze(1).to_broadcast([128, KEYS, 3, GP]),
                                        ALU.mult).then_inc(C_hot, 1)

            def add(sp, q):
                n = len(span(q)) * P
                part = accT[:, q * PER_BANK * P:q * PER_BANK * P + n]
                dve.wait_ge(C_o, sp * 7 + (q + 1 + FREE_O))
                dve.wait_ge(C_add, sp * 7 + (q + 1))
                nc.vector.tensor_tensor(part, part, ps[:, 5 + q % 3, 0:n], ALU.add).then_inc(C_add, 1)

            def column(s, par, ng, behind):
                for g in range(ng):
                    build(s * 5 + g, (par + g) % 2)
                    if g and behind:
                        for q in products_in(ng, g - 1):
                            add(s - 1, q)
                    if g == 0 and behind == 2:
                        for q in products_in(5, 4):
                            add(s - 2, q)

            columns_loop(dve, column)
            for q in products_in(LAST_G, LAST_G - 1):
                add(LAST - 1, q)
            for q in range(BANKFULS):
                add(LAST, q)

        def general_sums(dve, l):

            def link(ins):
                ins.then_inc(g_chain, 1)
                g_steps[0] += 1
                dve.wait_ge(g_chain, g_steps[0])

            if l == 0:
                dve.wait_ge(g_in, 48)
                for ids, parts, m in ((src_i, src_hl, T), (dst_i, dst_tl, P)):
                    link(nc.vector.tensor_copy(parts[:, 1, :], ids))
                    link(nc.vector.tensor_scalar(parts[:, 0, :], parts[:, 1, :], -(m - 1) / 2, 1.0 / m, ALU.add, ALU.mult))
                    link(nc.vector.tensor_scalar(parts[:, 0, :], parts[:, 0, :], ROUND, -ROUND, ALU.add, ALU.add))
                    link(nc.vector.scalar_tensor_tensor(parts[:, 1, :], parts[:, 0, :], -float(m), parts[:, 1, :], ALU.mult, ALU.add))
            dve.sem_inc(g_msg[l], 1)
            g_i = src_i if l < L else dst_i
            row, blk = (dst_tl[:, 1, :], dst_tl[:, 0, :]) if l < L else (src_hl[:, 0, :], src_hl[:, 1, :])
            with dve.Fori(0, K) as k:
                nc.vector.tensor_copy(gidx, g_i[:, bass.ds(k, 1)]).then_inc(g_idx[l], 1)
                nc.vector.tensor_copy(aidx, dst_i[:, bass.ds(k, 1)]).then_inc(g_idx[l], 1)
                dve.wait_ge(g_used[l], k + 1)
                nc.vector.tensor_scalar(oh_row, iota_f[0:P, 0:P], row[:, bass.ds(k, 1)], None, ALU.is_equal).then_inc(g_hot[l], 1)
                nc.vector.tensor_scalar(oh_blk, iota_f[0:P, 0:T], blk[:, bass.ds(k, 1)], None, ALU.is_equal).then_inc(g_hot[l], 1)
                dve.wait_ge(g_hot[l], k * 2 + 2)
                nc.vector.tensor_tensor(onehot, oh_row.unsqueeze(1).to_broadcast([P, T, P]), oh_blk.unsqueeze(2).to_broadcast([P, T, P]),
                                        ALU.mult).then_inc(g_oh[l], 1)
                if l < L:
                    dve.wait_ge(g_score[l], k + 1)
                    nc.vector.tensor_scalar(oh_s, oh_blk, score, None, ALU.mult)
                    nc.vector.tensor_scalar(msg, rows[:, 0:D], score, None, ALU.mult).then_inc(g_msg[l], 1)
                else:
                    dve.wait_ge(g_rows[l], k * 16 + 16)
                    nc.vector.tensor_scalar(msg, rows[:, 0:D], wgt[:, bass.ds(k, 1)], None, ALU.mult).then_inc(g_msg[l], 1)
            dve.wait_ge(g_used[l], K + 1)
            if l == L:
                dve.sem_inc(C_back, BANKFULS)
                return
            for q in range(BANKFULS):
                t = span(q)
                nc.vector.tensor_copy(accum[:, t.start:t.stop, :], ps[0:P, q, 0:len(t) * D].rearrange("p (t d) -> p t d", d=D))
            link(nc.vector.tensor_copy(general_scores, ps[0:P, 7, 0:T]))
            for j in range(NJ):
                finish_mean(dve, link, l, j, [(accum[:, j * JT:(j + 1) * JT, :], general_scores[:, j * JT:(j + 1) * JT], j * JT, JT)], B_ev[l])
                finish_residual(dve, link, l, j)
                finish_norm(dve, link, l, j)
                finish_outer(dve, l, j)

        @block.vector
        def _(dve):
            steps = [0]

            def link(ins):
                ins.then_inc(dchain, 1)
                steps[0] += 1
                dve.wait_ge(dchain, steps[0])

            dve.wait_ge(wins_ok, 1)
            dve.wait_ge(samp_in, 16)
            link(nc.vector.tensor_scalar(samp[:], samp_i[:, :, 0], 1.0 / WIN, None, ALU.mult))
            nc.vector.memset(ones16[:], 1.0).then_inc(consts, 1)
            for b in range(T):
                nc.vector.tensor_scalar(cmp_[:, b, :], wins, samp[:, b:b + 1], None, ALU.is_gt).then_inc(cmp_ok, 1)
            link(nc.vector.memset(ones[:], 1.0))
            link(nc.vector.memset(mv[:].rearrange("p a t c -> p (a t c)"), 0.0))
            dve.wait_ge(iotas, 3)
            link(nc.vector.tensor_copy(iota_f[:], small_i[:]))
            link(nc.vector.tensor_copy(part[:], part_i[:]))
            link(nc.vector.tensor_copy(first_t[:], win_i[:]))
            link(nc.vector.tensor_scalar(ident[:], iota_f[:], part[:], None, ALU.is_equal))
            link(nc.vector.tensor_copy(ident16[:], ident[:]))
            dve.sem_inc(consts, 1)
            dve.wait_ge(row_ps, 1)
            for i in (0, 1):
                w0, w1 = COUNT_SPLIT[i]
                last = nc.vector.tensor_copy(count_row[:, w0:w1], ps[0:1, 4 + i, 0:w1 - w0])
            last.then_inc(row_sb, 1)
            dve.wait_ge(cnt_ok, 1)
            link(nc.vector.tensor_scalar(bidx_f[:], ps[0:P, 7, 0:COLS], -1.0, 0.0, ALU.add, ALU.max))
            nc.vector.tensor_scalar(bidx[:], bidx_f[:], float(LASTB), None, ALU.min).then_inc(bidx_ok, 1)
            dve.wait_ge(w_in, LOADS)
            for l in range(L):
                link(nc.vector.tensor_tensor_reduce(prod, wideN[:, l, 0:D], wa2[:, l, :], 1.0, 0.0, ALU.mult, ALU.add, wideN[:, l, B:B + 1]))
                link(nc.vector.tensor_tensor_reduce(prod[0:P, :], biasN[:, l, 0:D], wa2[0:P, l, :], 1.0, 0.0, ALU.mult, ALU.add, biasN[:, l, B:B + 1]))
                link(nc.vector.memset(wideN[:, l, ONE:ONE + 1], 0.0))
                link(nc.vector.memset(biasN[:, l, ONE:ONE + 1], 1.0))
                link(nc.vector.memset(wa1_rep[:, l, :], 1.0))
                nc.vector.tensor_scalar(wa1_rep[:, l, :], wa1_rep[:, l, :], wa1[:, l:l + 1], None, ALU.mult).then_inc(wide_ok, 1)

            def nodes(l):
                for q in range(0, BANKFULS, 2):
                    n = len(span(q)) * P
                    dve.wait_ge(xt_ps, l * BANKFULS + q + 1)
                    nc.vector.tensor_copy(xT[:, q * PER_BANK * P:q * PER_BANK * P + n], ps[:, q, 0:n]).then_inc(xt_sv, 1)
                if l == L:
                    return
                for u in range(NBU):
                    n = min(3, T - 3 * u)
                    dve.wait_ge(nb_ps, l * (NBU + BANKFULS) + u + 1)
                    nc.vector.tensor_tensor(NB[:, 3 * u:3 * u + n, :], ps[0:P, u % 7, 0:n * NW].rearrange("p (t d) -> p t d", d=NW),
                                            biasN[:, l, :].unsqueeze(1).to_broadcast([P, n, NW]), ALU.add).then_inc(nb_sb, 1)
                for q in range(BANKFULS):
                    u, t = NBU + q, span(q)
                    dve.wait_ge(nb_ps, l * (NBU + BANKFULS) + u + 1)
                    nc.vector.tensor_tensor(so[:, t.start:t.stop, :], ps[0:P, u % 7, 0:len(t) * D].rearrange("p (t d) -> p t d", d=D),
                                            biasS[:, l, :].unsqueeze(1).to_broadcast([P, len(t), D]), ALU.add).then_inc(nb_sb, 1)

            nodes(0)

            f0, f1, f2, f3 = e_f[:4]
            dve.wait_ge(as_float, 1)
            link(nc.vector.tensor_scalar(f1, f0, -(T - 1) / 2, 1.0 / T, ALU.add, ALU.mult))
            nc.vector.tensor_scalar(f1, f1, ROUND, -ROUND, ALU.add, ALU.add).then_inc(hi_ok, 1)
            dve.wait_ge(hi_ok, 1)
            link(nc.vector.scalar_tensor_tensor(f0, f1, -float(T), f0, ALU.mult, ALU.add))
            dve.wait_ge(as_float, 2)
            nc.vector.tensor_tensor(f2, f2, first_t[:].unsqueeze(2).to_broadcast([P, COLS, SLOTS]), ALU.subtract).then_inc(delta_ok, 1)
            dve.wait_ge(delta_ok, 1)
            nc.vector.scalar_tensor_tensor(e_16[1], f2, float(T), f0, ALU.mult, ALU.add).then_inc(prep_ok[1], 1)
            dve.wait_ge(square_ok, 1)
            nc.vector.tensor_scalar(f3, f3, WIN * WIN / 4, 0.0, ALU.is_lt, ALU.add, accum_out=caught[:]).then_inc(caught_ok, 1)

            dve.wait_ge(et_sb, 4)
            dve.wait_ge(reps, 2)

            count_onehots = count_onehots_on(dve)
            first_groups(dve, count_onehots, MIX["vector"], LEAD)
            dve.wait_ge(et_sb, 10)
            dve.wait_ge(sum_ps, 1)
            nc.vector.tensor_scalar(fast_i[:], ps[0:1, 7, 0:1], float(E), None, ALU.is_equal).then_inc(flag_ok, 1)

            fast = is_fast(dve)
            for l in range(PASSES):
                if l:
                    nodes(l)
                if l == L:
                    dve.wait_ge(h_sb, BANKFULS)
                    link(nc.vector.memset(accT, 0.0))
                linked = steps[0]
                with dve.If(fast == 1):
                    if l < L:
                        attention_weights(dve, l, link, count_onehots if l == 0 else None)
                    else:
                        last_onehots(dve)
                linked = steps[0] - linked
                with dve.If(fast == 0):
                    general_sums(dve, l)
                    if linked:
                        dve.sem_inc(dchain, linked)

            dve.wait_ge(x1_in, 16)
            for q in range(BANKFULS + 1):
                if q < BANKFULS:
                    t = span(q)
                    m, n = USES[L][q], len(t)
                    y = so[:, t.start:t.stop, :]
                    dve.wait_ge(C_back, q + 1)
                    link(nc.vector.tensor_tensor(y, ps[0:P, q, 0:n * D].rearrange("p (t d) -> p t d", d=D),
                                                 bi1[:].unsqueeze(1).to_broadcast([P, n, D]), ALU.add))
                    link(nc.vector.scalar_tensor_tensor(y, y, 0.0, tmp[:, t.start:t.stop, :], ALU.max, ALU.add))
                    statistics(dve, link, y, m, n)
                if q:
                    t = span(q - 1)
                    normalise(dve, so[:, t.start:t.stop, :], USES[L][q - 1], len(t)).then_inc(fin_ok, 1)


_INS = ['x', 'src', 'dst', 'edge_weight', 'L0_gnn_Ws', 'L0_gnn_bs', 'L0_gnn_Wn', 'L0_gnn_bn', 'L0_gnn_Wa', 'L0_gnn_ba',
        'L0_gnn_gamma', 'L0_gnn_beta', 'L1_gnn_kernel', 'L1_gnn_bias']


def kernel(**inputs):
    import numpy as _np
    import concourse.bacc as _bacc
    from concourse import mybir as _mybir
    from concourse.bass_utils import run_bass_kernel_spmd as _run

    nc = _bacc.Bacc("TRN2", target_bir_lowering=False, num_devices=1)
    arrays, args = {}, []
    for name in _INS:
        a = _np.ascontiguousarray(inputs[name])
        arrays[f"in_{name}_dram"] = a
        args.append(nc.dram_tensor(f"in_{name}_dram", a.shape, _mybir.dt.from_np(a.dtype), kind="ExternalInput").ap())
    out = nc.dram_tensor("out_dram", (3125, 128), _mybir.dt.float32, kind="ExternalOutput").ap()
    gnn_kernel(nc, *args, out)
    r = _run(nc, [arrays], core_ids=[0])
    return r.results[0]["out_dram"]
```
